# Optimizing a Trainium2 kernel written in Bass

```python
import numpy as np
import jax
import jax.numpy as jnp

def _softmax(x, axis=-1):
    return jax.nn.softmax(x, axis=axis)

def _gelu(x):
    return jax.nn.gelu(x, approximate=True)

def _silu(x):
    return jax.nn.silu(x)

def _sigmoid(x):
    return jax.nn.sigmoid(x)

def _layernorm(x, axis=-1, eps=1e-05):
    m = jnp.mean(x, axis=axis, keepdims=True)
    v = jnp.var(x, axis=axis, keepdims=True)
    return (x - m) / jnp.sqrt(v + eps)

def _scatter_add(tgt, idx, src, axis=0):
    return tgt.at[idx].add(src)

def _segment_sum(src, seg, n):
    return jax.ops.segment_sum(src, seg, n)
kernel_name = 'mk_decoder_preln_d1_seqx_r8_279111'

def setup_inputs(seed: int=0):
    np.random.seed(seed)
    _w = jnp.asarray

    def _rec_inputs():
        import jax
        import jax.numpy as jnp
        _rk = jax.random.key(seed)
        x = 7.22e-05 + 1 * jax.random.normal(jax.random.fold_in(_rk, 1), (16, 100, 128), jnp.float32)
        _lenS = 100 - jax.random.randint(jax.random.fold_in(_rk, 7), (16,), 0, max(1, 100 // 4) + 1, jnp.int32)
        _lenS2 = 1444 - jax.random.randint(jax.random.fold_in(_rk, 8), (16,), 0, max(1, 1444 // 4) + 1, jnp.int32)
        _ctx_768P = jax.random.normal(jax.random.fold_in(_rk, 11), (16, 16, 96), jnp.float32)
        _ctx_768c = jax.random.dirichlet(jax.random.fold_in(_rk, 511), 0.3 * jnp.ones((16,), jnp.float32), (16, 1444))
        _ctx_768t = jnp.einsum('bsk,bkd->bsd', _ctx_768c, _ctx_768P)
        _ctx_768t = _ctx_768t * jax.lax.rsqrt(jnp.mean(jnp.square(_ctx_768t)) + 1e-12) * 0.953939
        ctx_768 = 2.09791e-05 + 1.00001 * (_ctx_768t + 0.3 * jax.random.normal(jax.random.fold_in(_rk, 611), (16, 1444, 96), jnp.float32))
        return (x, ctx_768)
    x, ctx_768 = _rec_inputs()

    def _L0_attn_setup():
        import jax, jax.numpy as jnp
        import numpy as np
        B, M, D = (4, 256, 128)

        def _rope_tables(m, d):
            i = jnp.arange(d // 2, dtype=jnp.float32)
            phi = jnp.power(10000.0, -2.0 * (i - 1.0) / d)
            pos = jnp.arange(m, dtype=jnp.float32)
            ang = pos[:, None] * phi[None, :]
            return (jnp.cos(ang), jnp.sin(ang))

        def _apply_rope(t, cos, sin):
            te = t[..., 0::2]
            to = t[..., 1::2]
            oe = te * cos + to * sin
            oo = -te * sin + to * cos
            return jnp.stack([oe, oo], axis=-1).reshape(t.shape)
        key = jax.random.key(seed)
        k1, k2, k3, k4 = jax.random.split(key, 4)
        x = jax.random.normal(k1, (B, M, D), dtype=jnp.float32)
        scale = 0.02
        wq = jax.random.normal(k2, (D, D), dtype=jnp.float32) * scale
        wk = jax.random.normal(k3, (D, D), dtype=jnp.float32) * scale
        wv = jax.random.normal(k4, (D, D), dtype=jnp.float32) * scale
        return {'x': x, 'wq': wq, 'wk': wk, 'wv': wv}
    _L0_attn_all = _L0_attn_setup()
    _L0_attn_in = {k: v for k, v in _L0_attn_all.items() if k in ('wq', 'wk', 'wv')}
    del _L0_attn_all

    def _L0_xattn_setup():
        import jax, jax.numpy as jnp
        import numpy as np
        HEADS = 16
        DIM_HEAD = 64
        key = jax.random.key(seed)
        ks = jax.random.split(key, 7)
        B, Nq, Dq = (4, 256, 128)
        Nk, Dc = (128, 96)
        inner = HEADS * DIM_HEAD
        sq = 1.0 / np.sqrt(Dq)
        sc = 1.0 / np.sqrt(Dc)
        si = 1.0 / np.sqrt(inner)
        return {'x': jax.random.normal(ks[0], (B, Nq, Dq), dtype=jnp.float32), 'context': jax.random.normal(ks[1], (B, Nk, Dc), dtype=jnp.float32), 'Wq': jax.random.normal(ks[2], (Dq, inner), dtype=jnp.float32) * sq, 'Wk': jax.random.normal(ks[3], (Dc, inner), dtype=jnp.float32) * sc, 'Wv': jax.random.normal(ks[4], (Dc, inner), dtype=jnp.float32) * sc, 'Wo': jax.random.normal(ks[5], (inner, Dq), dtype=jnp.float32) * si, 'bo': jax.random.normal(ks[6], (Dq,), dtype=jnp.float32) * 0.01}
    _L0_xattn_all = _L0_xattn_setup()
    _L0_xattn_in = {k: v for k, v in _L0_xattn_all.items() if k in ('Wq', 'Wk', 'Wv', 'Wo', 'bo')}
    del _L0_xattn_all

    def _L0_ffn_setup():
        import jax, jax.numpy as jnp
        import numpy as np
        B, S, D_IN, D_OUT = (16, 512, 128, 128)
        ACT_BITS = 8
        QB = float(2 ** (ACT_BITS - 1) - 1)
        key = jax.random.key(seed)
        k1, k2, k3 = jax.random.split(key, 3)
        x = jax.random.normal(k1, (B, S, D_IN), dtype=jnp.float32)
        ternary_weight = jax.random.randint(k2, (D_OUT, D_IN), 0, 3, dtype=jnp.int32)
        bias = jax.random.normal(k3, (D_OUT,), dtype=jnp.float32)
        act_scale = (jnp.max(jnp.abs(x)) / QB).astype(jnp.float32)
        return {'x': x, 'ternary_weight': ternary_weight, 'bias': bias, 'act_scale': act_scale}
    _L0_ffn_all = _L0_ffn_setup()
    _L0_ffn_in = {k: v for k, v in _L0_ffn_all.items() if k in ('ternary_weight', 'bias', 'act_scale')}
    del _L0_ffn_all
    return {'x': x, 'ctx_768': ctx_768, 'L0_attn_wq': _L0_attn_in['wq'], 'L0_attn_wk': _L0_attn_in['wk'], 'L0_attn_wv': _L0_attn_in['wv'], 'L0_xattn_Wq': _L0_xattn_in['Wq'], 'L0_xattn_Wk': _L0_xattn_in['Wk'], 'L0_xattn_Wv': _L0_xattn_in['Wv'], 'L0_xattn_Wo': _L0_xattn_in['Wo'], 'L0_xattn_bo': _L0_xattn_in['bo'], 'L0_ffn_ternary_weight': _L0_ffn_in['ternary_weight'], 'L0_ffn_bias': _L0_ffn_in['bias'], 'L0_ffn_act_scale': _L0_ffn_in['act_scale']}

def reference(x, ctx_768, L0_attn_wq, L0_attn_wk, L0_attn_wv, L0_xattn_Wq, L0_xattn_Wk, L0_xattn_Wv, L0_xattn_Wo, L0_xattn_bo, L0_ffn_ternary_weight, L0_ffn_bias, L0_ffn_act_scale):
    import jax
    import jax.numpy as jnp

    def _L0_attn_ref(x, wq, wk, wv):
        import jax, jax.numpy as jnp
        import numpy as np
        B, M, D = (4, 256, 128)

        def _rope_tables(m, d):
            i = jnp.arange(d // 2, dtype=jnp.float32)
            phi = jnp.power(10000.0, -2.0 * (i - 1.0) / d)
            pos = jnp.arange(m, dtype=jnp.float32)
            ang = pos[:, None] * phi[None, :]
            return (jnp.cos(ang), jnp.sin(ang))

        def _apply_rope(t, cos, sin):
            te = t[..., 0::2]
            to = t[..., 1::2]
            oe = te * cos + to * sin
            oo = -te * sin + to * cos
            return jnp.stack([oe, oo], axis=-1).reshape(t.shape)
        b, m, d = x.shape
        q = x @ wq.T
        k = x @ wk.T
        v = x @ wv.T
        cos, sin = _rope_tables(m, d)
        qr = _apply_rope(q, cos, sin)
        kr = _apply_rope(k, cos, sin)
        scores = jnp.einsum('bqd,bkd->bqk', qr, kr) / jnp.sqrt(jnp.float32(d))
        causal = jnp.tril(jnp.ones((m, m), dtype=bool))
        scores = jnp.where(causal[None, :, :], scores, jnp.finfo(scores.dtype).min)
        attn = jax.nn.softmax(scores, axis=-1)
        return jnp.einsum('bqk,bkd->bqd', attn, v)

    def _L0_xattn_ref(x, context, Wq, Wk, Wv, Wo, bo):
        import jax, jax.numpy as jnp
        import numpy as np
        HEADS = 16
        DIM_HEAD = 64
        B, Nq, _ = x.shape
        Nk = context.shape[1]
        h, dh = (HEADS, DIM_HEAD)
        q = (x @ Wq).reshape(B, Nq, h, dh)
        k = (context @ Wk).reshape(B, Nk, h, dh)
        v = (context @ Wv).reshape(B, Nk, h, dh)
        scale = 1.0 / jnp.sqrt(jnp.asarray(dh, dtype=x.dtype))
        scores = jnp.einsum('bqhd,bkhd->bhqk', q, k) * scale
        attn = jax.nn.softmax(scores, axis=-1)
        out = jnp.einsum('bhqk,bkhd->bqhd', attn, v).reshape(B, Nq, h * dh)
        return out @ Wo + bo

    def _L0_ffn_ref(x, ternary_weight, bias, act_scale):
        import jax, jax.numpy as jnp
        import numpy as np
        B, S, D_IN, D_OUT = (16, 512, 128, 128)
        ACT_BITS = 8
        QB = float(2 ** (ACT_BITS - 1) - 1)
        scale = jnp.maximum(act_scale, 1e-05)
        x_int = jnp.clip(jnp.round(x / scale), -QB, QB)
        x_dq = jnp.nan_to_num(x_int * scale, nan=0.0, posinf=10000.0, neginf=-10000.0)
        w = ternary_weight.astype(jnp.float32) - 1.0
        return jnp.einsum('bsi,oi->bso', x_dq, w) + bias
    x = x + _L0_attn_ref(_layernorm(x, axis=-1), L0_attn_wq, L0_attn_wk, L0_attn_wv)
    x = x + _L0_xattn_ref(_layernorm(x, axis=-1), ctx_768, L0_xattn_Wq, L0_xattn_Wk, L0_xattn_Wv, L0_xattn_Wo, L0_xattn_bo)
    x = x + _L0_ffn_ref(_layernorm(x, axis=-1), L0_ffn_ternary_weight, L0_ffn_bias, L0_ffn_act_scale)
    return x

_drawn_inputs = setup_inputs


def setup_inputs(seed=0):
    import zlib

    import numpy as np

    out = dict(_drawn_inputs(seed))
    spreads = {}
    factors = {'L0_attn_wq': 8.0, 'L0_attn_wk': 8.0, 'L0_xattn_bo': 4.075}
    for name, (base, spread) in spreads.items():
        noise = np.random.default_rng([zlib.crc32(name.encode()), seed]).standard_normal(out[name].shape)
        drawn = base * np.exp(spread * noise) if base else spread * noise
        out[name] = jnp.asarray(drawn.astype(out[name].dtype))
    for name, factor in factors.items():
        out[name] = (out[name] * factor).astype(out[name].dtype)
    return out
```

```python
from contextlib import ExitStack

import concourse.bass as bass
from concourse import mybir


def decoder_layer(nc, x_in, ctx_in, ctxT_in, wself_in, wqT_in, wkT_in, wvT_in, wo_in, bo_in,
                  tern_in, fbias_in, ascale_in, cos_in, sin_in, out):
    F32, F32R, I32 = mybir.dt.float32, mybir.dt.float32r, mybir.dt.int32
    ALU, ACT, AX = mybir.AluOpType, mybir.ActivationFunctionType, mybir.AxisListType

    B, S, D = x_in.shape
    NK, DC = ctx_in.shape[1:]
    DH, H, _ = wqT_in.shape
    T = B * S
    P = nc.NUM_PARTITIONS
    Q = H * S
    NCH = -(-NK // P)
    FULL = NK // P
    REST = NK - FULL * P
    BLK = 4 * S
    PAIR = 2 * BLK
    NP = Q // PAIR
    STEPS = NP * NCH
    LAG = 2
    RING = 3
    QT = -(-Q // P)
    PIECES = 3
    PW = 482
    PAT = [0, PW, NK - PW]
    QB = H // 4
    PARTS = 4
    EPS = 1e-5
    MAGIC = 1.5 * 2.0 ** 23
    QMAX = 127.0
    FLT_MAX = 3.4028234663852886e38
    LOOPED = 12
    assert STEPS % RING == 0 and STEPS % 2 == 0 and Q % PAIR == 0 and BLK <= 512

    with ExitStack() as stack:
        def sb(name, shape, dt=F32):
            return stack.enter_context(nc.sbuf_tensor(name, shape, dt))

        def two(name, shape, dt=F32):
            return [sb(f"{name}{i}", shape, dt) for i in range(2)]

        def sem(name):
            return stack.enter_context(nc.semaphore(name))

        X = sb("X", [S, B, D])
        M_hi = sb("M_hi", [D, H, DC], F32R)
        M_lo = sb("M_lo", [D, H, DC], F32R)
        G = sb("G", [DC, H, D])
        wqT = sb("wqT", [DH, H, D])
        wkT = sb("wkT", [DH, H, DC])
        wvT = sb("wvT", [DH, H, DC])
        wo = sb("wo", [DH, H, D])
        ident = sb("ident", [P, P])
        wself = sb("wself", [D, 5, D])
        cosT = sb("cosT", [D, S])
        sinT = sb("sinT", [D, S])
        mask = sb("mask", [S, S])
        bo_bc = sb("bo_bc", [S, D])
        fb_bc = sb("fb_bc", [S, D])
        tern = sb("tern", [D, D], I32)
        wffn = sb("wffn", [D, D])
        scl = sb("scl", [S, 4])
        eps = sb("eps", [S, 1])
        minus_half = sb("minus_half", [S, 1])
        q_hi = two("q_hi", [DC + 1, Q], F32R)
        q_lo = two("q_lo", [DC, Q], F32R)
        cT_hi = two("cT_hi", [DC + 1, NCH * P], F32R)
        cT_lo = two("cT_lo", [DC, NCH * P], F32R)
        cN_hi = two("cN_hi", [P, NCH, DC + 2], F32R)
        cN_lo = two("cN_lo", [P, NCH, DC], F32R)
        cT_raw = sb("cT_raw", [DC, NK])
        cN_raw = sb("cN_raw", [P, NCH, DC])
        pr = sb("pr", [P, 2, PAIR])
        pr_hi = sb("pr_hi", [P, RING, PAIR], F32R)
        pr_lo = sb("pr_lo", [P, RING, PAIR], F32R)
        maxes = sb("maxes", [P, QT, PIECES])
        negmax = sb("negmax", [P, QT])
        negmaxT = sb("negmaxT", [QT, P], F32R)
        sums = sb("sums", [H, S])
        rsums = sb("rsums", [H, S])
        o_sb = sb("o_sb", [DC + 1, Q])
        rrow = sb("rrow", [1, Q])
        rball = sb("rball", [DC, Q])
        st1, st2, st3 = (sb(f"st{i}", [S, 6]) for i in (1, 2, 3))
        mv1, mv2, mv3 = (sb(f"mv{i}", [S, 2]) for i in (1, 2, 3))
        ve1, ve2, ve3 = (sb(f"ve{i}", [S, 1]) for i in (1, 2, 3))
        rs1, rs2, rs3 = (sb(f"rs{i}", [S, 1]) for i in (1, 2, 3))
        xn1 = two("xn1", [S, D])
        xnT = two("xnT", [D, S])
        rt = sb("rt", [D, 2, S])
        rt2 = sb("rt2", [D, 2, S])
        qk = two("qk", [D, 2, S])
        V = two("V", [S, D])
        sc = two("sc", [S, S])
        nsmax = two("nsmax", [S, 1])
        ssum = two("ssum", [S, 1])
        rsum = two("rsum", [S, 1])
        prT = two("prT", [S, S])
        x1 = two("x1", [S, D])
        xn2 = two("xn2", [S, D])
        x2T_hi = two("x2T_hi", [D, S], F32R)
        x2T_lo = two("x2T_lo", [D, S], F32R)
        x2 = sb("x2", [S, D])
        x2b = sb("x2b", [S, D])
        xq = sb("xq", [S, D])
        xneg = sb("xneg", [S, D])
        xdT = sb("xdT", [D, S])
        result = two("result", [S, D])

        banks = stack.enter_context(nc.psum_tensor("banks", [P, 8, 512], F32))
        ST, OUT, MISC = 0, 4, 6

        block = stack.enter_context(nc.Block())

        x_in_s, x_rest_s = sem("x_in_s"), sem("x_rest_s")
        w_in_s, small_in_s = sem("w_in_s"), sem("small_in_s")
        ctx_in_s = sem("ctx_in_s")
        row_in_s = sem("row_in_s")
        sums_in_s = sem("sums_in_s")
        rrow_in_s = sem("rrow_in_s")
        out_s = sem("out_s")
        const_s = sem("const_s")
        mg_ready = sem("mg_ready")
        st_ready = sem("st_ready")
        pv_done = sem("pv_done")
        misc_ready = sem("misc_ready")
        max0_ready = sem("max0_ready")
        mhi_done, g_done = sem("mhi_done"), sem("g_done")
        exp_done, hi_done = sem("exp_done"), sem("hi_done")
        o_evac = sem("o_evac")
        qhi_done = sem("qhi_done")
        cThi_done, cNhi_done = sem("cThi_done"), sem("cNhi_done")
        sexp_done = sem("sexp_done")
        x2hi_done = sem("x2hi_done")
        vchain = sem("vchain")
        mlo_done = sem("mlo_done")
        lo_done = sem("lo_done")
        misc_free = sem("misc_free")
        max0_done = sem("max0_done")
        negmax_done, recip_done = sem("negmax_done"), sem("recip_done")
        rope_done, smax_done = sem("rope_done"), sem("smax_done")
        stats_done = [sem(f"stats{i}_done") for i in (1, 2, 3)]
        xn1_done, xn2_done, xd_done = sem("xn1_done"), sem("xn2_done"), sem("xd_done")
        wffn_done = sem("wffn_done")
        pchain = sem("pchain")
        cTlo_done, cNlo_done, on_done = sem("cTlo_done"), sem("cNlo_done"), sem("on_done")
        rstd_done = [sem(f"rstd{i}_done") for i in (1, 2, 3)]
        x1b_done, x2b_done = sem("x1b_done"), sem("x2b_done")

        def at_least(eng, s, value):
            if not isinstance(value, int) or value > 0:
                eng.wait_ge(s, value)

        SELF = ("T1", "QK", "V", "S", "PT", "AO", "T2")
        START = [("T1", 0), ("T1", 1), ("QK", 0), ("V", 0), ("QK", 1), ("V", 1), ("S", 0), ("S", 1),
                 ("PT", 0), ("PT", 1), ("AO", 0), ("AO", 1), ("T2", 0), ("T2", 1)]
        NSTART = len(START) + QB + 1
        MAX_END = 21
        AT = {s: [] for s in range(STEPS)}
        for what, s in zip(SELF[:-1], (3, 4, 5, 6, 9, 10)):
            AT[s].append((what, 0, 2))
        for s in range(2, MAX_END):
            for k in range(-(-(s - 2) * QT * PIECES // (MAX_END - 2)), -(-(s - 1) * QT * PIECES // (MAX_END - 2))):
                AT[s].append(("max", k, 1))
        AT[MAX_END].append(("negmax", 0, 1))
        for what, s in (("T3", 19), ("F", 21)):
            AT[s].append((what, 0, -1))
        LATE = ("q", "y", "T2")
        for j in range(QB):
            AT[2 * j].append(("q", j, 1))
        AT[12].append(("y", 0, -1))
        AT[15].append(("T2", 0, 2))

        def present(b, away):
            return not isinstance(b, int) or 0 <= b + away < B

        def length(b):
            return sum(present(b, away) for items in AT.values() for _, _, away in items)

        FULLBODY = sum(len(items) for items in AT.values())
        assert FULLBODY % 2 == 0

        def base(b):
            if isinstance(b, int):
                return NSTART + sum(length(i) for i in range(b))
            return NSTART + length(0) - FULLBODY + b * FULLBODY

        def body_uses(b):
            k, found = 0, []
            parity = base(b if isinstance(b, int) else 1)
            for items in AT.values():
                found.append([])
                for what, j, away in items:
                    if present(b, away):
                        found[-1].append((what, j, away, base(b) + k, MISC + (parity + k) % 2))
                        k += 1
            return found

        def use_of(b, wanted):
            return next(use for step in body_uses(b) for what, _, _, use, _ in step if what == wanted)

        def batches(eng, body):
            body(0, 0)
            with eng.Fori(0, LOOPED // 2) as i:
                for h in (0, 1):
                    body(i * 2 + (1 + h), 1 - h)
            for b in range(LOOPED + 1, B):
                body(b, b % 2)

        def qtile(t):
            return min(t * P, Q - P)

        class Order:

            def __init__(self, eng, s, each):
                self.eng, self.s, self.each = eng, s, each
                self.count = 0
                self.at = 0

            def enter(self, b):
                if isinstance(b, int):
                    if b == LOOPED + 1:
                        self.count += LOOPED * self.each
                    else:
                        self.count += self.at
                    self.base = self.count
                else:
                    if self.at and not hasattr(self, "looped"):
                        self.count += self.at
                        self.looped = True
                    elif self.at != self.each:
                        raise ValueError(f"a looped batch has {self.at} links")
                    self.base = self.count + (b - 1) * self.each
                self.at = 0

            def mark(self, ins):
                ins.then_inc(self.s, 1)
                self.at += 1

            def wait(self):
                self.eng.wait_ge(self.s, self.base + self.at)

            def link(self, ins):
                self.mark(ins)
                self.wait()

        GBANKS = [4, 5, 0, 1]

        @block.sync
        def _(sp):
            sp.dma_start(X[:, 0:2, :], x_in[0:2, :, :].rearrange("b s d -> s b d")).then_inc(x_in_s, 16)
            for dst, src in ((wself[:, :, :], wself_in), (cosT[:, :], cos_in), (sinT[:, :], sin_in)):
                sp.dma_start(dst, src).then_inc(small_in_s, 16)
            for dst, src in ((wqT, wqT_in), (wkT, wkT_in), (wvT, wvT_in), (wo, wo_in)):
                sp.dma_start(dst[:, :, :], src).then_inc(w_in_s, 16)

            def load_ctx(n):
                sp.dma_start(cT_raw[:, :], ctxT_in[n, :, :]).then_inc(ctx_in_s, 16)
                sp.dma_start(cN_raw[:, 0:FULL, :],
                             ctx_in[n, 0:FULL * P, :].rearrange("(p j) d -> p j d", j=FULL)).then_inc(ctx_in_s, 16)
                sp.dma_start(cN_raw[0:REST, FULL, :], ctx_in[n, FULL * P:NK, :]).then_inc(ctx_in_s, 16)

            load_ctx(0)
            for dst, src in ((bo_bc[:, :], bo_in.rearrange("(a d) -> a d", a=1).to_broadcast([S, D])),
                             (fb_bc[:, :], fbias_in.rearrange("(a d) -> a d", a=1).to_broadcast([S, D])),
                             (tern[:, :], tern_in), (scl[:, 0:1], ascale_in.to_broadcast([S, 1]))):
                sp.dma_start(dst, src).then_inc(small_in_s, 16)
            sp.dma_start(X[:, 2:B, :], x_in[2:B, :, :].rearrange("b s d -> s b d")).then_inc(x_rest_s, 16)

            def split_done(n):
                sp.wait_ge(cThi_done, 2 * (n + 1))
                sp.wait_ge(cNhi_done, n + 1)
                sp.wait_ge(cTlo_done, n + 1)
                sp.wait_ge(cNlo_done, n + 1)

            def move_negmax(n, par, use):
                sp.wait_ge(misc_free, use + 1)
                full = Q // P
                sp.dma_start(q_hi[par][DC:DC + 1, 0:full * P].bitcast(F32),
                             negmaxT[0:full, :].bitcast(F32)).then_inc(row_in_s, 16)
                sp.dma_start(q_hi[par][DC:DC + 1, full * P:Q].bitcast(F32),
                             negmaxT[full:QT, P - (Q - full * P):P].bitcast(F32)).then_inc(row_in_s, 16)

            def move_sums(n):
                sp.wait_ge(o_evac, NP * (n + 1))
                sp.dma_start(sums[:, :], o_sb[DC:DC + 1, :].rearrange("p (h s) -> p h s", h=H)).then_inc(sums_in_s, 16)
                sp.wait_ge(recip_done, n + 1)
                sp.dma_start(rrow[:, :].rearrange("p (h s) -> p h s", h=H), rsums[:, :]).then_inc(rrow_in_s, 16)

            def store(n, par, use):
                sp.wait_ge(misc_free, use + 1)
                sp.dma_start(out[n, :, :], result[par][:, :]).then_inc(out_s, 16)

            split_done(0)
            load_ctx(1)
            move_negmax(0, 0, NSTART - 1)

            def body(b, par):
                ahead = b + 2 if isinstance(b, int) else sp.snap(b + 2)
                before = b - 1 if isinstance(b, int) else sp.snap(b - 1)
                if present(b, -1):
                    move_sums(b - 1)
                if present(b, 2):
                    split_done(b + 1)
                    load_ctx(ahead)
                if present(b, -1):
                    store(before, 1 - par, use_of(b, "F"))
                if present(b, 1):
                    move_negmax(b + 1, 1 - par, use_of(b, "negmax"))

            batches(sp, body)
            move_sums(B - 1)
            store(B - 1, 1, base(B) + 2)
            sp.wait_ge(out_s, 16 * B)

        NCONST = 4 + 2 * 7

        @block.gpsimd
        def _(pool):
            nc.gpsimd.memset(ident[:, :], 0.0).then_inc(pchain, 1)
            nc.gpsimd.memset(mask[:, :], 0.0).then_inc(pchain, 1)
            pool.wait_ge(pchain, 2)
            nc.gpsimd.affine_select(out=ident[:, :], in_=ident[:, :], compare_op=ALU.not_equal, fill=1.0,
                                    base=0, pattern=[[-1, P]], channel_multiplier=1).then_inc(const_s, 1)
            nc.gpsimd.affine_select(out=mask[:, :], in_=mask[:, :], compare_op=ALU.is_ge, fill=-FLT_MAX,
                                    base=0, pattern=[[-1, S]], channel_multiplier=1).then_inc(const_s, 1)
            nc.gpsimd.memset(eps[:, :], EPS).then_inc(const_s, 1)
            nc.gpsimd.memset(minus_half[:, :], -0.5).then_inc(const_s, 1)
            made = [4]
            pool.wait_ge(const_s, 4)

            def constant(view, value):
                nc.gpsimd.memset(view.bitcast(F32), value).then_inc(const_s, 1)
                made[0] += 1
                pool.wait_ge(const_s, made[0])

            def padding(i):
                constant(cT_hi[i][:, NK:NCH * P], 0.0)
                constant(cT_lo[i][:, NK:NCH * P], 0.0)
                constant(cN_hi[i][:, FULL, :], 0.0)
                constant(cN_lo[i][:, FULL, :], 0.0)
                constant(cT_hi[i][DC:DC + 1, 0:NK], 1.0)
                constant(cN_hi[i][:, 0:FULL, DC:DC + 2], 1.0)
                constant(cN_hi[i][0:REST, FULL, DC:DC + 2], 1.0)

            order = Order(pool, pchain, 4)
            order.count = 2
            order.base = 2

            def power(i, n, ve, mv, rs):
                pool.wait_ge(stats_done[i], n + 1)
                order.link(nc.gpsimd.tensor_tensor(out=ve[:, :], in0=mv[:, 1:2], in1=eps[:, :], op=ALU.add))
                nc.gpsimd.tensor_tensor(out=rs[:, :], in0=ve[:, :], in1=minus_half[:, :],
                                        op=ALU.pow).then_inc(rstd_done[i], 1)

            def residual(n, par):
                nc.gpsimd.tensor_tensor(out=X[:, bass.ds(n, 1), :].rearrange("p a d -> p (a d)"), in0=x1[par][:, :], in1=bo_bc[:, :],
                                        op=ALU.add).then_inc(x1b_done, 1)

            def split_T(n, par, rows_in=0):
                pool.wait_ge(cThi_done, 2 * (n + 1))
                at_least(pool, st_ready, (n - 1) * STEPS)
                half = NK // 2
                nc.gpsimd.tensor_tensor(out=cT_lo[par][:, 0:half], in0=cT_raw[:, 0:half],
                                        in1=cT_hi[par][0:DC, 0:half].bitcast(F32), op=ALU.subtract)
                at_least(pool, rrow_in_s, rows_in * 16)
                nc.gpsimd.tensor_tensor(out=cT_lo[par][:, half:NK], in0=cT_raw[:, half:NK],
                                        in1=cT_hi[par][0:DC, half:NK].bitcast(F32), op=ALU.subtract).then_inc(cTlo_done, 1)

            def split_N(n, par):
                pool.wait_ge(cNhi_done, n + 1)
                at_least(pool, pv_done, (n - 1) * STEPS)
                nc.gpsimd.tensor_tensor(out=cN_lo[par][:, 0:FULL, :], in0=cN_raw[:, 0:FULL, :],
                                        in1=cN_hi[par][:, 0:FULL, 0:DC].bitcast(F32), op=ALU.subtract)
                nc.gpsimd.tensor_tensor(out=cN_lo[par][0:REST, FULL, :], in0=cN_raw[0:REST, FULL, :],
                                        in1=cN_hi[par][0:REST, FULL, 0:DC].bitcast(F32), op=ALU.subtract).then_inc(cNlo_done, 1)

            def normalize(n):
                if isinstance(n, int):
                    pool.wait_ge(rrow_in_s, (n + 1) * 16)
                order.link(nc.gpsimd.partition_broadcast(rball[:, :], rrow[:, :]))
                nc.gpsimd.tensor_tensor(out=o_sb[0:DC, :], in0=o_sb[0:DC, :], in1=rball[:, :],
                                        op=ALU.mult).then_inc(on_done, 1)

            def ffn_input(n):
                power(2, n, ve3, mv3, rs3)
                nc.gpsimd.tensor_tensor(out=x2b[:, :], in0=x2[:, :], in1=fb_bc[:, :], op=ALU.add).then_inc(x2b_done, 1)

            for n in (0, 1):
                power(0, n, ve1, mv1, rs1)
            padding(0)
            split_T(0, 0)
            split_N(0, 0)
            pool.wait_ge(small_in_s, 16 * 7)
            for n in (0, 1):
                power(1, n, ve2, mv2, rs2)
                residual(n, n)
            padding(1)

            def body(b, par):
                order.enter(b)
                if present(b, 2):
                    power(0, b + 2, ve1, mv1, rs1)
                if present(b, 1):
                    split_T(b + 1, 1 - par, b if present(b, -1) else 0)
                if present(b, -1):
                    normalize(b - 1)
                if present(b, 1):
                    split_N(b + 1, 1 - par)
                if present(b, 2):
                    power(1, b + 2, ve2, mv2, rs2)
                    residual(b + 2, par)
                if present(b, -1):
                    ffn_input(b - 1)

            batches(pool, body)
            order.enter(B)
            normalize(B - 1)
            ffn_input(B - 1)

        @block.scalar
        def _(act):
            def self_exp(n, par):
                act.wait_ge(smax_done, n + 1)
                nc.scalar.activation(sc[par][:, :], sc[par][:, :], ACT.Exp, bias=nsmax[par][:, :],
                                     accum_out=ssum[par][:, :]).then_inc(sexp_done, 1)

            def high_x2(n, par, use, bank):
                act.wait_ge(misc_ready, use + 1)
                nc.scalar.activation(x2T_hi[par][:, :], banks[:, bank, 0:S], ACT.Copy).then_inc(x2hi_done, 1)

            def high_N(n, par, part):
                if part == 0:
                    act.wait_ge(ctx_in_s, (n + 1) * 48)
                    at_least(act, pv_done, (n - 1) * STEPS)
                if part < PARTS - 1:
                    chunks = slice(part * FULL // (PARTS - 1), (part + 1) * FULL // (PARTS - 1))
                    nc.scalar.activation(cN_hi[par][:, chunks, 0:DC], cN_raw[:, chunks, :], ACT.Copy)
                else:
                    nc.scalar.activation(cN_hi[par][0:REST, FULL, 0:DC], cN_raw[0:REST, FULL, :],
                                         ACT.Copy).then_inc(cNhi_done, 1)

            def high_q(n, par, j, use, bank):
                act.wait_ge(misc_ready, use + 1)
                nc.scalar.activation(q_hi[par][0:DC, j * BLK:(j + 1) * BLK], banks[0:DC, bank, 0:BLK],
                                     ACT.Copy).then_inc(qhi_done, 1)

            def evacuate(n, pair, y_use=None):
                act.wait_ge(pv_done, n * STEPS + (pair + 1) * NCH)
                if y_use is not None:
                    act.wait_ge(misc_ready, y_use + 1)
                nc.scalar.activation(o_sb[:, pair * PAIR:(pair + 1) * PAIR].rearrange("p (a q) -> p a q", a=2),
                                     banks[0:DC + 1, OUT:OUT + 2, 0:BLK], ACT.Copy).then_inc(o_evac, 1)

            def g_bank(j):
                act.wait_ge(mg_ready, 5 + j)
                nc.scalar.activation(G[:, 4 * j:4 * j + 4, :],
                                     banks[0:DC, GBANKS[j], :].rearrange("p (h d) -> p h d", h=4),
                                     ACT.Copy).then_inc(g_done, 1)

            for j in range(4):
                act.wait_ge(mg_ready, j + 1)
                nc.scalar.activation(M_hi[:, 4 * j:4 * j + 4, :],
                                     banks[:, j, 0:4 * DC].rearrange("p (h d) -> p h d", h=4),
                                     ACT.Copy).then_inc(mhi_done, 1)
            act.wait_ge(const_s, NCONST // 2 + 2)
            for part in range(PARTS):
                high_N(0, 0, part)
            for j in range(2):
                g_bank(j)
            for n in range(2):
                self_exp(n, n)
            for j in range(2, 4):
                g_bank(j)
            for n in range(2):
                high_x2(n, n, START.index(("T2", n)), MISC + START.index(("T2", n)) % 2)
            for j in range(QB):
                high_q(0, 0, j, len(START) + j, MISC + (len(START) + j) % 2)
            act.wait_ge(const_s, NCONST)

            def body(b, par):
                at = body_uses(b)
                for s in range(STEPS):
                    n = b * STEPS + s
                    pair = banks[:, ST + 2 * (s % 2):ST + 2 * (s % 2) + 2, 0:BLK]
                    act.wait_ge(st_ready, n + 1)
                    at_least(act, lo_done, n - 1)
                    nc.scalar.activation(pr[:, s % 2, :].rearrange("p (a q) -> p a q", a=2), pair, ACT.Exp,
                                         scale=float(DH) ** -0.5).then_inc(exp_done, 1)
                    at_least(act, pv_done, n - RING + 1)
                    nc.scalar.activation(pr_hi[:, s % RING, :].rearrange("p (a q) -> p a q", a=2), pair, ACT.Exp,
                                         scale=float(DH) ** -0.5).then_inc(hi_done, 1)
                    if s == LAG - 1 and present(b, -1):
                        evacuate(b - 1, NP - 1)
                    if s == NCH + LAG - 1:
                        evacuate(b, 0, use_of(b, "y") if present(b, -1) else None)
                    for what, j, away, use, bank in at[s]:
                        if what == "q":
                            high_q(b + 1, 1 - par, j, use, bank)
                        elif what == "T2":
                            high_x2(b + 2, par, use, bank)
                    if present(b, 1) and 4 <= s < 4 + PARTS:
                        high_N(b + 1, 1 - par, s - 4)
                    if s == 7 and present(b, 2):
                        self_exp(b + 2, par)

            batches(act, body)
            evacuate(B - 1, NP - 1)

        @block.vector
        def _(dve):
            order = Order(dve, vchain, 10)
            order.base = 0
            link = order.link

            def stats(st, x):
                order.mark(nc.vector.bn_stats(st[:, :], x))

            def aggregate(i, st, mv):
                nc.vector.bn_aggr(mv[:, :], st[:, :]).then_inc(stats_done[i], 1)

            def normalized(i, n, dst, x, mv, rs, done):
                dve.wait_ge(rstd_done[i], n + 1)
                return nc.vector.tensor_scalar(dst, x, mv[:, 0:1], rs[:, :], ALU.subtract, ALU.mult).then_inc(done, 1)

            def row(n):
                return X[:, bass.ds(n, 1), :].rearrange("p a d -> p (a d)")

            def consume(n, par, what, j, use, bank):
                dve.wait_ge(misc_ready, use + 1)
                here = banks[:, bank, :]
                if what == "q":
                    dve.wait_ge(qhi_done, n * QB + j + 1)
                    nc.vector.tensor_tensor(q_lo[par][:, j * BLK:(j + 1) * BLK], here[0:DC, 0:BLK],
                                            q_hi[par][0:DC, j * BLK:(j + 1) * BLK].bitcast(F32),
                                            ALU.subtract).then_inc(misc_free, 1)
                elif what == "max":
                    t, p = divmod(j, PIECES)
                    nc.vector.tensor_reduce(maxes[:, t, p:p + 1], here[:, 0:PW], AX.X,
                                            ALU.max).then_inc(misc_free, 1)
                    if j == QT * PIECES - 1:
                        dve.wait_ge(misc_free, use + 1)
                        nc.vector.tensor_reduce(negmax[:, :], maxes[:, :, :], AX.X, ALU.max,
                                                negate=True).then_inc(negmax_done, 1)
                elif what == "negmax":
                    at_least(dve, row_in_s, n * 32)
                    nc.vector.tensor_copy(negmaxT[:, :], here[0:QT, 0:P]).then_inc(misc_free, 1)
                elif what == "T1":
                    nc.vector.tensor_copy(xnT[par][:, :], here[:, 0:S]).then_inc(misc_free, 1)
                elif what == "QK":
                    v = here[:, 0:4 * S].rearrange("p (a m s) -> p a m s", a=2, m=2)
                    at_least(dve, rope_done, n)
                    order.mark(nc.vector.tensor_tensor(rt[:, :, :], v[:, :, 0, :],
                                                       cosT[:, :].unsqueeze(1).to_broadcast([D, 2, S]), ALU.mult))
                    nc.vector.tensor_tensor(rt2[:, :, :], v[:, :, 1, :],
                                            sinT[:, :].unsqueeze(1).to_broadcast([D, 2, S]),
                                            ALU.mult).then_inc(misc_free, 1)
                    dve.wait_ge(misc_free, use + 1)
                    order.wait()
                    nc.vector.tensor_tensor(qk[par][:, :, :], rt[:, :, :], rt2[:, :, :], ALU.add).then_inc(rope_done, 1)
                elif what == "V":
                    nc.vector.tensor_copy(V[par][:, :], here[0:S, 0:D]).then_inc(misc_free, 1)
                elif what == "S":
                    nc.vector.scalar_tensor_tensor(out=sc[par][:, :], in0=here[0:S, 0:S], scalar=float(D) ** -0.5,
                                                   in1=mask[:, :], op0=ALU.mult, op1=ALU.add).then_inc(misc_free, 1)
                    dve.wait_ge(misc_free, use + 1)
                    nc.vector.tensor_reduce(nsmax[par][:, :], sc[par][:, :], AX.X, ALU.max,
                                            negate=True).then_inc(smax_done, 1)
                elif what == "PT":
                    nc.vector.tensor_copy(prT[par][:, :], here[0:S, 0:S]).then_inc(misc_free, 1)
                    dve.wait_ge(sexp_done, n + 1)
                    order.mark(nc.vector.reciprocal(rsum[par][:, :], ssum[par][:, :]))
                elif what == "AO":
                    order.wait()
                    nc.vector.scalar_tensor_tensor(out=x1[par][:, :], in0=here[0:S, 0:D], scalar=rsum[par][:, :],
                                                   in1=row(n), op0=ALU.mult, op1=ALU.add).then_inc(misc_free, 1)
                    dve.wait_ge(misc_free, use + 1)
                    stats(st2, x1[par][:, :])
                elif what == "T2":
                    dve.wait_ge(x2hi_done, n + 1)
                    nc.vector.tensor_tensor(x2T_lo[par][:, :], here[:, 0:S], x2T_hi[par][:, :].bitcast(F32),
                                            ALU.subtract).then_inc(misc_free, 1)
                elif what == "y":
                    dve.wait_ge(x1b_done, n + 1)
                    nc.vector.tensor_tensor(x2[:, :], here[0:S, 0:D], row(n), ALU.add).then_inc(misc_free, 1)
                    dve.wait_ge(misc_free, use + 1)
                    stats(st3, x2[:, :])
                elif what == "T3":
                    nc.vector.tensor_copy(xdT[:, :], here[:, 0:S]).then_inc(misc_free, 1)
                elif what == "F":
                    dve.wait_ge(x2b_done, n + 1)
                    at_least(dve, out_s, n * 16)
                    nc.vector.tensor_tensor(result[par][:, :], here[0:S, 0:D], x2b[:, :], ALU.add).then_inc(misc_free, 1)

            def quantize(part):
                if part == 0:
                    order.wait()
                    link(nc.vector.tensor_scalar(xneg[:, :], xq[:, :], scl[:, 3:4], 0.0, ALU.mult, ALU.min))
                    link(nc.vector.tensor_scalar(xq[:, :], xq[:, :], scl[:, 3:4], 0.0, ALU.mult, ALU.max))
                elif part == 1:
                    link(nc.vector.scalar_tensor_tensor(out=xq[:, :], in0=xq[:, :], scalar=QMAX, in1=xneg[:, :],
                                                        op0=ALU.min, op1=ALU.add))
                    link(nc.vector.tensor_scalar(xq[:, :], xq[:, :], -QMAX, MAGIC, ALU.max, ALU.add))
                else:
                    nc.vector.tensor_scalar(xq[:, :], xq[:, :], MAGIC, scl[:, 2:3], ALU.subtract,
                                            ALU.mult).then_inc(xd_done, 1)

            def high_T(n, par, half):
                if half == 0:
                    dve.wait_ge(ctx_in_s, (n + 1) * 48)
                    at_least(dve, st_ready, (n - 1) * STEPS)
                keys = slice(half * NK // 2, (half + 1) * NK // 2)
                nc.vector.tensor_copy(cT_hi[par][0:DC, keys], cT_raw[:, keys]).then_inc(cThi_done, 1)

            def normalize3(n):
                dve.wait_ge(rstd_done[2], n + 1)
                order.mark(nc.vector.tensor_scalar(xq[:, :], x2[:, :], mv3[:, 0:1], rs3[:, :], ALU.subtract, ALU.mult))

            def start(what, n):
                k = START.index((what, n))
                consume(n, n, what, 0, k, MISC + k % 2)

            dve.wait_ge(x_in_s, 16)
            for n in (0, 1):
                if n:
                    dve.wait_ge(rstd_done[0], 1)
                    dve.wait_ge(xn1_done, 1)
                stats(st1, X[:, n, :])
                order.wait()
                aggregate(0, st1, mv1)
                normalized(0, n, xn1[n][:, :], X[:, n, :], mv1, rs1, xn1_done)
            for what, n in START[:2]:
                start(what, n)
            for j in range(4):
                dve.wait_ge(mhi_done, j + 1)
                nc.vector.tensor_tensor(M_lo[:, 4 * j:4 * j + 4, :],
                                        banks[:, j, 0:4 * DC].rearrange("p (h d) -> p h d", h=4),
                                        M_hi[:, 4 * j:4 * j + 4, :].bitcast(F32), ALU.subtract).then_inc(mlo_done, 1)
            dve.wait_ge(const_s, NCONST // 2 + 2)
            high_T(0, 0, 0)
            high_T(0, 0, 1)
            dve.wait_ge(small_in_s, 16 * 7)
            for what, n in START[2:10]:
                start(what, n)
            order.wait()
            for n in (0, 1):
                if n:
                    dve.wait_ge(rstd_done[1], 1)
                    dve.wait_ge(xn2_done, 1)
                start("AO", n)
                order.wait()
                aggregate(1, st2, mv2)
                normalized(1, n, xn2[n][:, :], x1[n][:, :], mv2, rs2, xn2_done)
            start("T2", 0)
            start("T2", 1)
            nc.vector.tensor_scalar(wffn[:, :], tern[:, :], 1.0, None, ALU.subtract).then_inc(wffn_done, 1)
            link(nc.vector.tensor_scalar(scl[:, 1:2], scl[:, 0:1], 0.0, None, ALU.mult))
            link(nc.vector.tensor_scalar(scl[:, 3:4], scl[:, 0:1], 1e-5, scl[:, 1:2], ALU.max, ALU.add))
            link(nc.vector.reciprocal(scl[:, 3:4], scl[:, 3:4]))
            link(nc.vector.tensor_scalar(scl[:, 2:3], scl[:, 0:1], 1e-5, FLT_MAX, ALU.max, ALU.min))
            for j in range(QB):
                k = len(START) + j
                consume(0, 0, "q", j, k, MISC + k % 2)
            for t in range(QT):
                dve.wait_ge(max0_ready, t + 1)
                nc.vector.tensor_reduce(maxes[:, t, 0:1], banks[:, PIECES * (t % 2):PIECES * (t % 2) + PIECES, 0:PW],
                                        AX.XY, ALU.max).then_inc(max0_done, 1)
            dve.wait_ge(max0_done, QT)
            nc.vector.tensor_scalar(negmax[:, :], maxes[:, :, 0], -1.0, None, ALU.mult).then_inc(negmax_done, 1)
            consume(0, 0, "negmax", 0, NSTART - 1, MISC + (NSTART - 1) % 2)
            dve.wait_ge(x_rest_s, 16)

            def body(b, par):
                at = body_uses(b)
                order.enter(b)
                for s in range(STEPS):
                    n = b * STEPS + s
                    whats = [what for what, *_ in at[s]]
                    if s < 2 and present(b, 1):
                        high_T(b + 1, 1 - par, s)
                    if present(b, 2):
                        if s == 0:
                            stats(st1, row(b + 2))
                        if s == 2:
                            normalized(0, b + 2, xn1[par][:, :], row(b + 2), mv1, rs1, xn1_done)
                        if s == 12:
                            normalized(1, b + 2, xn2[par][:, :], x1[par][:, :], mv2, rs2, xn2_done)
                    if present(b, -1):
                        if s == 15:
                            normalize3(b - 1)
                        if 16 <= s <= 18:
                            quantize(s - 16)
                    for what, j, away, use, bank in at[s]:
                        if what not in LATE:
                            consume(b + away, par if away == 2 else 1 - par, what, j, use, bank)
                    y_before = s > 0 and "y" in [what for what, *_ in at[s - 1]]
                    if s == 0 or "AO" in whats or y_before:
                        order.wait()
                    dve.wait_ge(exp_done, n + 1)
                    dve.wait_ge(hi_done, n + 1)
                    at_least(dve, pv_done, n - RING + 1)
                    nc.vector.tensor_tensor(pr_lo[:, s % RING, :], pr[:, s % 2, :],
                                            pr_hi[:, s % RING, :].bitcast(F32), ALU.subtract).then_inc(lo_done, 1)
                    if s == 0 and present(b, 2):
                        aggregate(0, st1, mv1)
                    if "AO" in whats:
                        aggregate(1, st2, mv2)
                    if y_before:
                        aggregate(2, st3, mv3)
                    if s == 3 and present(b, -1):
                        dve.wait_ge(sums_in_s, b * 16)
                        nc.vector.reciprocal(rsums[:, :], sums[:, :]).then_inc(recip_done, 1)
                    for what, j, away, use, bank in at[s]:
                        if what in LATE:
                            consume(b + away, par if away == 2 else 1 - par, what, j, use, bank)

            batches(dve, body)
            order.enter(B)
            dve.wait_ge(sums_in_s, B * 16)
            nc.vector.reciprocal(rsums[:, :], sums[:, :]).then_inc(recip_done, 1)
            consume(B - 1, 1, "y", 0, base(B), MISC + base(B) % 2)
            order.wait()
            aggregate(2, st3, mv3)
            normalize3(B - 1)
            for part in range(3):
                quantize(part)
            consume(B - 1, 1, "T3", 0, base(B) + 1, MISC + (base(B) + 1) % 2)
            consume(B - 1, 1, "F", 0, base(B) + 2, MISC + (base(B) + 2) % 2)

        @block.tensor
        def _(pe):
            def fill(n, par, what, j, use, bank):
                at_least(pe, misc_free, use - 1)
                here = banks[:, bank, :]
                if what == "q":
                    for i in range(4):
                        h = 4 * j + i
                        o = here[0:DC, i * S:(i + 1) * S]
                        nc.tensor.matmul(o, M_hi[:, h, :], x2T_hi[par][:, :], start=True, stop=False)
                        nc.tensor.matmul(o, M_hi[:, h, :], x2T_lo[par][:, :], start=False, stop=False)
                        mm = nc.tensor.matmul(o, M_lo[:, h, :], x2T_hi[par][:, :], start=False, stop=True)
                elif what == "max":
                    t, p = divmod(j, PIECES)
                    if j == 0:
                        pe.wait_ge(cThi_done, 2 * (n + 1))
                    bank_of = [(qtile(i) + P - 1) // BLK for i in range(QT)]
                    if p == 0 and (t == 0 or bank_of[t] > bank_of[t - 1]):
                        pe.wait_ge(qhi_done, n * QB + bank_of[t] + 1)
                    mm = nc.tensor.matmul(here[:, 0:PW], q_hi[par][0:DC, qtile(t):qtile(t) + P],
                                          cT_hi[par][0:DC, PAT[p]:PAT[p] + PW], start=True, stop=True)
                elif what == "negmax":
                    pe.wait_ge(negmax_done, n + 1)
                    mm = nc.tensor.transpose(here[0:QT, 0:P], negmax[:, :], ident[:, :])
                elif what == "T1":
                    pe.wait_ge(xn1_done, n + 1)
                    mm = nc.tensor.transpose(here[:, 0:S], xn1[par][:, :], ident[0:S, 0:S])
                elif what == "QK":
                    pe.wait_ge(misc_free, use)
                    for m in range(4):
                        mm = nc.tensor.matmul(here[:, m * S:(m + 1) * S], wself[:, m, :], xnT[par][:, :],
                                              start=True, stop=True)
                elif what == "V":
                    mm = nc.tensor.matmul(here[0:S, 0:D], xnT[par][:, :], wself[:, 4, :], start=True, stop=True)
                elif what == "S":
                    pe.wait_ge(rope_done, n + 1)
                    mm = nc.tensor.matmul(here[0:S, 0:S], qk[par][:, 0, :], qk[par][:, 1, :], start=True, stop=True)
                elif what == "PT":
                    pe.wait_ge(sexp_done, n + 1)
                    mm = nc.tensor.transpose(here[0:S, 0:S], sc[par][:, :], ident[0:S, 0:S])
                elif what == "AO":
                    pe.wait_ge(misc_free, use)
                    mm = nc.tensor.matmul(here[0:S, 0:D], prT[par][:, :], V[par][:, :], start=True, stop=True)
                elif what == "T2":
                    pe.wait_ge(xn2_done, n + 1)
                    mm = nc.tensor.transpose(here[:, 0:S], xn2[par][:, :], ident[0:S, 0:S])
                elif what == "y":
                    pe.wait_ge(on_done, n + 1)
                    for h in range(H):
                        mm = nc.tensor.matmul(here[0:S, 0:D], o_sb[0:DC, h * S:(h + 1) * S], G[:, h, :],
                                              start=(h == 0), stop=(h == H - 1))
                elif what == "T3":
                    pe.wait_ge(xd_done, n + 1)
                    mm = nc.tensor.transpose(here[:, 0:S], xq[:, :], ident[0:S, 0:S])
                elif what == "F":
                    pe.wait_ge(misc_free, use)
                    mm = nc.tensor.matmul(here[0:S, 0:D], xdT[:, :], wffn[:, :], start=True, stop=True)
                mm.then_inc(misc_ready, 1)

            def start(what, n):
                k = START.index((what, n))
                fill(n, n, what, 0, k, MISC + k % 2)

            def m_banks():
                for j in range(4):
                    for i in range(4):
                        mm = nc.tensor.matmul(banks[:, j, i * DC:(i + 1) * DC], wqT[:, 4 * j + i, :],
                                              wkT[:, 4 * j + i, :], start=True, stop=True)
                    mm.then_inc(mg_ready, 1)

            def g_bank(j):
                if GBANKS[j] < 4:
                    pe.wait_ge(mlo_done, GBANKS[j] + 1)
                for i in range(4):
                    mm = nc.tensor.matmul(banks[0:DC, GBANKS[j], i * D:(i + 1) * D], wvT[:, 4 * j + i, :],
                                          wo[:, 4 * j + i, :], start=True, stop=True)
                mm.then_inc(mg_ready, 1)

            pe.wait_ge(const_s, 4)
            start("T1", 0)
            start("T1", 1)
            pe.wait_ge(w_in_s, 64)
            m_banks()
            pe.wait_ge(small_in_s, 16 * 7)
            for what, n in START[2:6]:
                start(what, n)
            g_bank(0)
            g_bank(1)
            start("S", 0)
            start("S", 1)
            g_bank(2)
            g_bank(3)
            for what, n in START[8:]:
                start(what, n)
            pe.wait_ge(mlo_done, 4)
            pe.wait_ge(g_done, 4)
            for j in range(QB):
                k = len(START) + j
                fill(0, 0, "q", j, k, MISC + k % 2)
            pe.wait_ge(cThi_done, 2)
            pe.wait_ge(qhi_done, QB)
            for t in range(QT):
                at_least(pe, max0_done, t - 1)
                for p in range(PIECES):
                    mm = nc.tensor.matmul(banks[:, PIECES * (t % 2) + p, 0:PW], q_hi[0][0:DC, qtile(t):qtile(t) + P],
                                          cT_hi[0][0:DC, PAT[p]:PAT[p] + PW], start=True, stop=True)
                mm.then_inc(max0_ready, 1)
            fill(0, 0, "negmax", 0, NSTART - 1, MISC + (NSTART - 1) % 2)
            pe.wait_ge(max0_done, QT)
            pe.wait_ge(wffn_done, 1)
            pe.wait_ge(const_s, NCONST)

            def scores(b, par, s, i):
                pair, c = divmod(s, NCH)
                if s == 0 and i == 0:
                    pe.wait_ge(row_in_s, (b + 1) * 32)
                    pe.wait_ge(cTlo_done, b + 1)
                if i == 0:
                    at_least(pe, hi_done, b * STEPS + s - 1)
                keys = slice(c * P, (c + 1) * P)
                terms = [(cT_hi[par][0:DC + 1, keys], q_hi[par][0:DC + 1, :]),
                         (cT_hi[par][0:DC, keys], q_lo[par][:, :]),
                         (cT_lo[par][:, keys], q_hi[par][0:DC, :])]
                k, q = terms[i]
                for a in range(2):
                    q0 = pair * PAIR + a * BLK
                    mm = nc.tensor.matmul(banks[:, ST + 2 * (s % 2) + a, 0:BLK], k, q[:, q0:q0 + BLK],
                                          start=(i == 0), stop=(i == 2))
                if i == 2:
                    mm.then_inc(st_ready, 1)

            def values(b, par, s, i):
                pair, c = divmod(s, NCH)
                if s == 0 and i == 0:
                    pe.wait_ge(cNhi_done, b + 1)
                    pe.wait_ge(cNlo_done, b + 1)
                if c == 0 and i == 0:
                    at_least(pe, o_evac, b * NP + pair)
                if i == 0:
                    pe.wait_ge(hi_done, b * STEPS + s + 1)
                if i == 2:
                    pe.wait_ge(lo_done, b * STEPS + s + 1)
                r = s % RING
                terms = [(cN_hi[par][:, c, 0:DC + 1], pr_hi, DC + 1), (cN_lo[par][:, c, :], pr_hi, DC),
                         (cN_hi[par][:, c, 0:DC + 1], pr_lo, DC + 1)]
                k, e, m = terms[i]
                for a in range(2):
                    mm = nc.tensor.matmul(banks[0:m, OUT + a, 0:BLK], k, e[:, r, a * BLK:(a + 1) * BLK],
                                          start=(c == 0 and i == 0), stop=(c == NCH - 1 and i == 2))
                if i == 2:
                    mm.then_inc(pv_done, 1)

            def body(b, par):
                at = body_uses(b)
                for s in range(STEPS):
                    for i in range(6):
                        if i < 3:
                            scores(b, par, s, i)
                        elif s >= LAG:
                            values(b, par, s - LAG, i - 3)
                        elif present(b, -1):
                            values(b - 1, 1 - par, STEPS + s - LAG, i - 3)
                        for what, j, away, use, bank in at[s][i * len(at[s]) // 6:(i + 1) * len(at[s]) // 6]:
                            fill(b + away, par if away == 2 else 1 - par, what, j, use, bank)

            batches(pe, body)
            for s in range(STEPS - LAG, STEPS):
                for i in range(3):
                    values(B - 1, 1, s, i)
            for k, what in enumerate(("y", "T3", "F")):
                fill(B - 1, 1, what, 0, base(B) + k, MISC + (base(B) + k) % 2)


def kernel(x, ctx_768, L0_attn_wq, L0_attn_wk, L0_attn_wv, L0_xattn_Wq, L0_xattn_Wk, L0_xattn_Wv,
           L0_xattn_Wo, L0_xattn_bo, L0_ffn_ternary_weight, L0_ffn_bias, L0_ffn_act_scale):
    import numpy as np
    import concourse.bacc as bacc
    from concourse.bass_utils import run_bass_kernel_spmd

    B, S, D = x.shape
    NK, DC = ctx_768.shape[1:]
    DH = 64
    H = L0_xattn_Wq.shape[1] // DH
    P = 128
    full = NK // P
    ctx = np.asarray(ctx_768)
    ctxT = np.concatenate([ctx[:, :full * P].reshape(B, P, full, DC).transpose(0, 3, 2, 1).reshape(B, DC, full * P),
                           ctx[:, full * P:].transpose(0, 2, 1)], axis=2)
    order = np.concatenate([np.arange(0, D, 2), np.arange(1, D, 2)])
    swapped = np.concatenate([order[D // 2:], order[:D // 2]])
    wq, wk, wv = (np.asarray(w) for w in (L0_attn_wq, L0_attn_wk, L0_attn_wv))
    wself = np.stack([wq[order].T, wq[swapped].T, wk[order].T, wk[swapped].T, wv.T], axis=1)
    i = np.arange(D // 2, dtype=np.float32)
    phi = np.power(np.float32(10000.0), np.float32(-2.0) * (i - np.float32(1.0)) / np.float32(D)).astype(np.float32)
    ang = (phi[:, None] * np.arange(S, dtype=np.float32)[None, :]).astype(np.float32)
    cos, sin = np.cos(ang).astype(np.float32), np.sin(ang).astype(np.float32)

    def by_head(w):
        return np.asarray(w).reshape(w.shape[0], H, DH).transpose(2, 1, 0)

    named = {
        "x": np.asarray(x), "ctx": ctx, "ctxT": ctxT, "wself": wself,
        "wqT": by_head(L0_xattn_Wq), "wkT": by_head(L0_xattn_Wk), "wvT": by_head(L0_xattn_Wv),
        "wo": np.asarray(L0_xattn_Wo).reshape(H, DH, D).transpose(1, 0, 2),
        "bo": np.asarray(L0_xattn_bo), "tern": np.asarray(L0_ffn_ternary_weight).T,
        "fbias": np.asarray(L0_ffn_bias), "ascale": np.asarray(L0_ffn_act_scale).reshape(1, 1),
        "cos": np.concatenate([cos, cos]), "sin": np.concatenate([sin, -sin]),
    }
    nc = bacc.Bacc("TRN2", target_bir_lowering=False, num_devices=1)
    arrays, args = {}, []
    for name, a in named.items():
        a = np.ascontiguousarray(a)
        arrays["in_" + name] = a
        args.append(nc.dram_tensor("in_" + name, a.shape, mybir.dt.from_np(a.dtype), kind="ExternalInput").ap())
    args.append(nc.dram_tensor("out", (B, S, D), mybir.dt.float32, kind="ExternalOutput").ap())
    decoder_layer(nc, *args)
    r = run_bass_kernel_spmd(nc, [arrays], core_ids=[0])
    return r.results[0]["out"]
```

```python
from contextlib import ExitStack

import concourse.bass as bass
from concourse import mybir


COPIES = [(0, 36, "hi"), (0, 28, "lo"), (0, 36, "hi"), (28, 8, "lo")]
LOW_AT = 64


def decoder_layer(nc, x_in, ctx_in, ctx_last_in, ctxT_in, wself_in, wqT_in, wkT_in, wvT_in, wo_in, bo_in,
                  tern_in, fbias_in, ascale_in, cos_in, sin_in, last_in, out):
    F32, F32R, I32 = mybir.dt.float32, mybir.dt.float32r, mybir.dt.int32
    ALU, ACT, AX = mybir.AluOpType, mybir.ActivationFunctionType, mybir.AxisListType

    B, S, D = x_in.shape
    NK, DC = ctx_in.shape[1:]
    DH, H, _ = wqT_in.shape
    T = B * S
    P = nc.NUM_PARTITIONS
    Q = H * S
    NCH = -(-NK // P)
    FULL = NK // P
    REST = NK - FULL * P
    ROWS = sum(keys for _, keys, _ in COPIES)
    NT = FULL * P + ROWS
    BLK = 4 * S
    PAIR = 2 * BLK
    NP = Q // PAIR
    STEPS = NP * NCH
    LAG = 2
    RING = 3
    QT = -(-Q // P)
    FIRST = -(-PAIR // P)
    PIECES = 3
    PW = 482
    PAT = [0, PW, NK - PW]
    QB = H // 4
    PARTS = 4
    EPS = 1e-5
    MAGIC = 1.5 * 2.0 ** 23
    QMAX = 127.0
    FLT_MAX = 3.4028234663852886e38
    LOOPED = B - 4
    assert STEPS % RING == 0 and STEPS % 2 == 0 and Q % PAIR == 0 and BLK <= 512
    assert sum(keys for _, keys, kind in COPIES if kind == "lo") == REST and ROWS <= P
    assert LOW_AT == sum(keys for _, keys, _ in COPIES[:2]) and COPIES[0][1] == COPIES[2][1] == REST

    with ExitStack() as stack:
        def sb(name, shape, dt=F32):
            return stack.enter_context(nc.sbuf_tensor(name, shape, dt))

        def two(name, shape, dt=F32):
            return [sb(f"{name}{i}", shape, dt) for i in range(2)]

        def sem(name):
            return stack.enter_context(nc.semaphore(name))

        X = sb("X", [S, B, D])
        M = sb("M", [D, H, DC])
        G = sb("G", [DC, H, D])
        wqT = sb("wqT", [DH, H, D])
        wkT = sb("wkT", [DH, H, DC])
        wvT = sb("wvT", [DH, H, DC])
        wo = sb("wo", [DH, H, D])
        ident = sb("ident", [P, P])
        wself = sb("wself", [D, 5, D])
        cosT = sb("cosT", [D, S])
        sinT = sb("sinT", [D, S])
        mask = sb("mask", [S, S])
        bo_bc = sb("bo_bc", [S, D])
        fb_bc = sb("fb_bc", [S, D])
        tern = sb("tern", [D, D], I32)
        wffn = sb("wffn", [D, D])
        scl = sb("scl", [S, 4])
        eps = sb("eps", [S, 1])
        minus_half = sb("minus_half", [S, 1])
        q_hi = two("q_hi", [DC + 1, Q], F32R)
        q_lo = two("q_lo", [DC, Q], F32R)
        cT_hi = two("cT_hi", [DC + 1, NCH * P], F32R)
        cT_lo = two("cT_lo", [DC, NCH * P], F32R)
        cN_hi = two("cN_hi", [P, NCH, DC + 2], F32R)
        cN_lo = two("cN_lo", [P, FULL, DC], F32R)
        last_hi = sb("last_hi", [ROWS, DC], F32R)
        last = sb("last", [P, 2])
        cT_raw = sb("cT_raw", [DC, NT])
        cN_raw = sb("cN_raw", [P, NCH, DC])
        pr = sb("pr", [P, 2, PAIR])
        pr_hi = sb("pr_hi", [P, RING, PAIR], F32R)
        pr_lo = sb("pr_lo", [P, RING, PAIR], F32R)
        maxes = sb("maxes", [P, QT, PIECES])
        negmax = sb("negmax", [P, QT])
        negmaxT = sb("negmaxT", [QT, P], F32R)
        sums = sb("sums", [H, S])
        rsums = sb("rsums", [H, S])
        o_sb = sb("o_sb", [DC + 1, Q])
        rrow = sb("rrow", [1, Q])
        rball = sb("rball", [DC, Q])
        st1, st2, st3 = (sb(f"st{i}", [S, 6]) for i in (1, 2, 3))
        mv1, mv2, mv3 = (sb(f"mv{i}", [S, 2]) for i in (1, 2, 3))
        ve1, ve2, ve3 = (sb(f"ve{i}", [S, 1]) for i in (1, 2, 3))
        rs1, rs2, rs3 = (sb(f"rs{i}", [S, 1]) for i in (1, 2, 3))
        xn1 = two("xn1", [S, D])
        xnT = two("xnT", [D, S])
        rt = sb("rt", [D, 2, S])
        rt2 = sb("rt2", [D, 2, S])
        qk = two("qk", [D, 2, S])
        V = two("V", [S, D])
        sc = two("sc", [S, S])
        nsmax = two("nsmax", [S, 1])
        ssum = two("ssum", [S, 1])
        rT = sb("rT", [S, H])
        acc = sb("acc", [S, D])
        rsum = two("rsum", [S, 1])
        prT = two("prT", [S, S])
        x1 = two("x1", [S, D])
        xn2 = two("xn2", [S, D])
        x2T = two("x2T", [D, S])
        x2 = sb("x2", [S, D])
        x2b = sb("x2b", [S, D])
        xq = sb("xq", [S, D])
        xneg = sb("xneg", [S, D])
        xdT = sb("xdT", [D, S])
        result = two("result", [S, D])

        banks = stack.enter_context(nc.psum_tensor("banks", [P, 8, 512], F32))
        ST, OUT, MISC = 0, 4, 6

        block = stack.enter_context(nc.Block())

        x_in_s, x_rest_s = sem("x_in_s"), sem("x_rest_s")
        self_in_s = sem("self_in_s")
        last_in_s = sem("last_in_s")
        wqk_in_s, wvo_in_s = sem("wqk_in_s"), sem("wvo_in_s")
        ffn_in_s = sem("ffn_in_s")
        ctx_in_s = sem("ctx_in_s")
        row_a_in_s = sem("row_a_in_s")
        row_in_s = sem("row_in_s")
        sums_in_s = sem("sums_in_s")
        rrow_in_s = sem("rrow_in_s")
        out_s = sem("out_s")
        const_s = sem("const_s")
        mg_ready = sem("mg_ready")
        st_ready = sem("st_ready")
        pv_done = sem("pv_done")
        misc_ready = sem("misc_ready")
        max0_ready = sem("max0_ready")
        m_done, g_done = sem("m_done"), sem("g_done")
        exp_done, hi_done = sem("exp_done"), sem("hi_done")
        o_evac = sem("o_evac")
        qhi_done = sem("qhi_done")
        cThi_done, cNhi_done = sem("cThi_done"), sem("cNhi_done")
        sexp_done = sem("sexp_done")
        vchain = sem("vchain")
        lo_done = sem("lo_done")
        misc_free = sem("misc_free")
        max0_done = sem("max0_done")
        last_done = sem("last_done")
        negmax_a_done = sem("negmax_a_done")
        negmax_done, recip_done = sem("negmax_done"), sem("recip_done")
        rope_done, smax_done = sem("rope_done"), sem("smax_done")
        stats_done = [sem(f"stats{i}_done") for i in (1, 2, 3)]
        xn1_done, xn2_done, xd_done = sem("xn1_done"), sem("xn2_done"), sem("xd_done")
        wffn_done = sem("wffn_done")
        pchain = sem("pchain")
        cTlo_done, cNlo_done, on_done = sem("cTlo_done"), sem("cNlo_done"), sem("on_done")
        rstd_done = [sem(f"rstd{i}_done") for i in (1, 2, 3)]
        x1b_done, x2b_done = sem("x1b_done"), sem("x2b_done")

        def at_least(eng, s, value):
            if not isinstance(value, int) or value > 0:
                eng.wait_ge(s, value)

        SELF = ("T1", "QK", "V", "S", "PT", "AO", "T2")
        START = [("T1", 0), ("T1", 1), ("QK", 0), ("V", 0), ("QK", 1), ("V", 1), ("S", 0), ("S", 1),
                 ("PT", 0), ("PT", 1), ("AO", 0), ("T2", 0)] + [("q", j) for j in range(QB)] + [
                 ("AO", 1), ("T2", 1), ("negmax_a", 0)]
        NSTART = len(START)
        INPUT = {"QK": ("T1",), "V": ("T1",), "AO": ("PT",), "q": ("T2",), "F": ("T3",)}
        GBANKS = [OUT, OUT + 1, MISC, MISC + 1]
        BETWEEN = {0: ("q", 2), 1: ("q", 3), 2: ("AO", 1), 4: ("T2", 1)}
        MAXES = [0, 2, 1, 1, 1, 2, 2, 3, 2, 3, 2, 2, 1, 4, 2, 1, 2, 1, 2, 2, 3]
        MAX_END = len(MAXES)
        AT = {s: [] for s in range(STEPS)}
        for what, s in zip(SELF[:-1], (3, 4, 5, 6, 8, 12)):
            AT[s].append((what, 0, 2))
        k = 0
        for s in range(1, MAX_END):
            for _ in range(MAXES[s]):
                AT[s].append(("max", k, 1))
                k += 1
        assert k == QT * PIECES
        AT[MAX_END].append(("negmax", 0, 1))
        for what, s in (("T3", 19), ("F", 20)):
            AT[s].append((what, 0, -1))
        LATE = ("q", "y")
        for j in range(QB):
            AT[(0, 3, 5, 8)[j]].append(("q", j, 1))
        AT[12].append(("y", 0, -1))
        AT[15].append(("T2", 0, 2))

        for s, what, j in ((16, "sums", 0), (17, "yh", 0), (19, "yh", 1)):
            AT[s].append((what, j, 0))
        BATCH_0 = ("max_b", "negmax_b")
        for k in range(FIRST * PIECES, QT * PIECES):
            AT[(k - FIRST * PIECES) // 2].append(("max_b", k, 0))
        AT[(QT - FIRST) * PIECES // 2].append(("negmax_b", 0, 0))
        for items in AT.values():
            items.sort(key=lambda item: item[0] in LATE)
        TAIL = [("sums", 1), ("yh", 2), ("yh", 3), ("T3", 0), ("F", 0)]

        def present(b, away, what=None):
            if away == 0:
                return isinstance(b, int) and b == (0 if what in BATCH_0 else B - 1)
            return not isinstance(b, int) or 0 <= b + away < B

        def length(b):
            return sum(present(b, away, what) for items in AT.values() for what, _, away in items)

        FULLBODY = sum(away != 0 for items in AT.values() for _, _, away in items)
        assert FULLBODY % 2 == 0

        def base(b):
            if isinstance(b, int):
                return NSTART + sum(length(i) for i in range(b))
            return NSTART + length(0) - FULLBODY + b * FULLBODY

        def body_uses(b):
            k, found = 0, []
            parity = base(b if isinstance(b, int) else 1)
            for items in AT.values():
                found.append([])
                for what, j, away in items:
                    if present(b, away, what):
                        found[-1].append((what, j, away, base(b) + k, MISC + (parity + k) % 2))
                        k += 1
            return found

        def use_of(b, wanted):
            return next(use for step in body_uses(b) for what, _, _, use, _ in step if what == wanted)

        def batches(eng, body):
            body(0, 0)
            with eng.Fori(0, LOOPED // 2) as i:
                for h in (0, 1):
                    body(i * 2 + (1 + h), 1 - h)
            for b in range(LOOPED + 1, B):
                body(b, b % 2)

        def chunk(s):
            return (s + FULL) % NCH

        def qtile(t):
            return min(t * P, Q - P)

        class Order:

            def __init__(self, eng, s, each):
                self.eng, self.s, self.each = eng, s, each
                self.count = 0
                self.at = 0
                self.looped = False

            def enter(self, b):
                if isinstance(b, int):
                    if b == LOOPED + 1:
                        self.count += LOOPED * self.each
                    else:
                        self.count += self.at
                    self.base = self.count
                else:
                    if not self.looped:
                        self.count += self.at
                        self.looped = True
                    elif self.at != self.each:
                        raise ValueError(f"a looped batch has {self.at} links")
                    self.base = self.count + (b - 1) * self.each
                self.at = 0

            def mark(self, ins):
                ins.then_inc(self.s, 1)
                self.at += 1

            def wait(self):
                self.eng.wait_ge(self.s, self.base + self.at)

            def link(self, ins):
                self.mark(ins)
                self.wait()

        @block.sync
        def _(sp):
            sp.dma_start(X[:, 0:2, :], x_in[0:2, :, :].rearrange("b s d -> s b d")).then_inc(x_in_s, 16)
            for dst, src in ((wself[:, :, :], wself_in), (cosT[:, :], cos_in), (sinT[:, :], sin_in)):
                sp.dma_start(dst, src).then_inc(self_in_s, 16)
            sp.dma_start(last[:, :], last_in).then_inc(last_in_s, 16)
            for dst, src in ((wqT, wqT_in), (wkT, wkT_in)):
                sp.dma_start(dst[:, :, :], src).then_inc(wqk_in_s, 16)

            def load_ctx(n):
                sp.dma_start(cT_raw[:, :], ctxT_in[n, :, :]).then_inc(ctx_in_s, 16)
                sp.dma_start(cN_raw[:, 0:FULL, :],
                             ctx_in[n, 0:FULL * P, :].rearrange("(p j) d -> p j d", j=FULL)).then_inc(ctx_in_s, 16)
                sp.dma_start(cN_raw[0:ROWS, FULL, :], ctx_last_in[n, :, :]).then_inc(ctx_in_s, 16)

            load_ctx(0)
            for dst, src in ((bo_bc[:, :], bo_in.rearrange("(a d) -> a d", a=1).to_broadcast([S, D])),
                             (fb_bc[:, :], fbias_in.rearrange("(a d) -> a d", a=1).to_broadcast([S, D])),
                             (tern[:, :], tern_in), (scl[:, 0:1], ascale_in.to_broadcast([S, 1]))):
                sp.dma_start(dst, src).then_inc(ffn_in_s, 16)
            for dst, src in ((wvT, wvT_in), (wo, wo_in)):
                sp.dma_start(dst[:, :, :], src).then_inc(wvo_in_s, 16)
            sp.dma_start(X[:, 2:B, :], x_in[2:B, :, :].rearrange("b s d -> s b d")).then_inc(x_rest_s, 16)

            def split_done(n):
                sp.wait_ge(cThi_done, 2 * (n + 1))
                sp.wait_ge(cNhi_done, n + 1)
                sp.wait_ge(cTlo_done, n + 1)
                sp.wait_ge(cNlo_done, n + 1)
                sp.wait_ge(last_done, n + 1)

            def move_negmax(n, par, use, first=0):
                sp.wait_ge(misc_free, use + 1)
                full = Q // P
                sp.dma_start(q_hi[par][DC:DC + 1, first * P:full * P].bitcast(F32),
                             negmaxT[0:full - first, :].bitcast(F32)).then_inc(row_in_s, 16)
                sp.dma_start(q_hi[par][DC:DC + 1, full * P:Q].bitcast(F32),
                             negmaxT[full - first:QT - first, P - (Q - full * P):P].bitcast(F32)).then_inc(row_in_s, 16)

            def move_sums(n):
                sp.wait_ge(o_evac, NP * (n + 1))
                sp.dma_start(sums[:, :], o_sb[DC:DC + 1, :].rearrange("p (h s) -> p h s", h=H)).then_inc(sums_in_s, 16)
                sp.wait_ge(recip_done, n + 1)
                sp.dma_start(rrow[:, :].rearrange("p (h s) -> p h s", h=H), rsums[:, :]).then_inc(rrow_in_s, 16)

            def store(n, par, use):
                sp.wait_ge(misc_free, use + 1)
                sp.dma_start(out[n, :, :], result[par][:, :]).then_inc(out_s, 16)

            split_done(0)
            load_ctx(1)
            sp.wait_ge(misc_free, NSTART)
            sp.dma_start(q_hi[0][DC:DC + 1, 0:FIRST * P].bitcast(F32),
                         negmaxT[0:FIRST, :].bitcast(F32)).then_inc(row_a_in_s, 16)

            def body(b, par):
                ahead = b + 2 if isinstance(b, int) else sp.snap(b + 2)
                before = b - 1 if isinstance(b, int) else sp.snap(b - 1)
                if present(b, 0, "negmax_b"):
                    move_negmax(0, 0, use_of(0, "negmax_b"), FIRST)
                if present(b, -1):
                    move_sums(b - 1)
                if present(b, 2):
                    split_done(b + 1)
                    load_ctx(ahead)
                if present(b, -1):
                    store(before, 1 - par, use_of(b, "F"))
                if present(b, 1):
                    move_negmax(b + 1, 1 - par, use_of(b, "negmax"))

            batches(sp, body)
            store(B - 1, 1, base(B) + TAIL.index(("F", 0)))
            sp.wait_ge(out_s, 16 * B)

        NCONST = 4 + 2 * 6

        @block.gpsimd
        def _(pool):
            nc.gpsimd.memset(ident[:, :], 0.0).then_inc(pchain, 1)
            nc.gpsimd.memset(mask[:, :], 0.0).then_inc(pchain, 1)
            pool.wait_ge(pchain, 2)
            nc.gpsimd.affine_select(out=ident[:, :], in_=ident[:, :], compare_op=ALU.not_equal, fill=1.0,
                                    base=0, pattern=[[-1, P]], channel_multiplier=1).then_inc(const_s, 1)
            nc.gpsimd.affine_select(out=mask[:, :], in_=mask[:, :], compare_op=ALU.is_ge, fill=-FLT_MAX,
                                    base=0, pattern=[[-1, S]], channel_multiplier=1).then_inc(const_s, 1)
            nc.gpsimd.memset(eps[:, :], EPS).then_inc(const_s, 1)
            nc.gpsimd.memset(minus_half[:, :], -0.5).then_inc(const_s, 1)
            made = [4]
            pool.wait_ge(const_s, 4)

            def constant(view, value):
                nc.gpsimd.memset(view.bitcast(F32), value).then_inc(const_s, 1)
                made[0] += 1
                pool.wait_ge(const_s, made[0])

            def padding(i):
                constant(cT_hi[i][:, NT:NCH * P], 0.0)
                constant(cT_lo[i][:, NT:NCH * P], 0.0)
                constant(cN_hi[i][:, FULL, :], 0.0)
                constant(cT_hi[i][DC:DC + 1, 0:NT], 1.0)
                constant(cN_hi[i][:, 0:FULL, DC:DC + 2], 1.0)
                pool.wait_ge(last_in_s, 16)
                nc.gpsimd.tensor_copy(cN_hi[i][:, FULL, DC:DC + 1], last[:, 1:2]).then_inc(const_s, 1)
                made[0] += 1
                pool.wait_ge(const_s, made[0])

            order = Order(pool, pchain, 4)
            order.count = 2
            order.base = 2

            def power(i, n, ve, mv, rs):
                pool.wait_ge(stats_done[i], n + 1)
                order.link(nc.gpsimd.tensor_tensor(out=ve[:, :], in0=mv[:, 1:2], in1=eps[:, :], op=ALU.add))
                nc.gpsimd.tensor_tensor(out=rs[:, :], in0=ve[:, :], in1=minus_half[:, :],
                                        op=ALU.pow).then_inc(rstd_done[i], 1)

            def residual(n, par):
                nc.gpsimd.tensor_tensor(out=X[:, bass.ds(n, 1), :].rearrange("p a d -> p (a d)"), in0=x1[par][:, :], in1=bo_bc[:, :],
                                        op=ALU.add).then_inc(x1b_done, 1)

            def split_T(n, par, rows_in=0):
                pool.wait_ge(cThi_done, 2 * (n + 1))
                at_least(pool, st_ready, (n - 1) * STEPS)
                half = NT // 2
                nc.gpsimd.tensor_tensor(out=cT_lo[par][:, 0:half], in0=cT_raw[:, 0:half],
                                        in1=cT_hi[par][0:DC, 0:half].bitcast(F32), op=ALU.subtract)
                at_least(pool, rrow_in_s, rows_in * 16)
                nc.gpsimd.tensor_tensor(out=cT_lo[par][:, half:NT], in0=cT_raw[:, half:NT],
                                        in1=cT_hi[par][0:DC, half:NT].bitcast(F32), op=ALU.subtract).then_inc(cTlo_done, 1)

            def split_N(n, par):
                pool.wait_ge(cNhi_done, n + 1)
                at_least(pool, pv_done, (n - 1) * STEPS)
                nc.gpsimd.tensor_tensor(out=cN_lo[par][:, :, :], in0=cN_raw[:, 0:FULL, :],
                                        in1=cN_hi[par][:, 0:FULL, 0:DC].bitcast(F32), op=ALU.subtract).then_inc(cNlo_done, 1)

            def normalize(n):
                if isinstance(n, int):
                    pool.wait_ge(rrow_in_s, (n + 1) * 16)
                order.link(nc.gpsimd.partition_broadcast(rball[:, :], rrow[:, :]))
                nc.gpsimd.tensor_tensor(out=o_sb[0:DC, :], in0=o_sb[0:DC, :], in1=rball[:, :],
                                        op=ALU.mult).then_inc(on_done, 1)

            def ffn_input(n):
                power(2, n, ve3, mv3, rs3)
                nc.gpsimd.tensor_tensor(out=x2b[:, :], in0=x2[:, :], in1=fb_bc[:, :], op=ALU.add).then_inc(x2b_done, 1)

            for n in (0, 1):
                power(0, n, ve1, mv1, rs1)
            padding(0)
            pool.wait_ge(ffn_in_s, 16 * 4)
            power(1, 0, ve2, mv2, rs2)
            residual(0, 0)
            split_T(0, 0)
            power(1, 1, ve2, mv2, rs2)
            residual(1, 1)
            split_N(0, 0)
            padding(1)

            def body(b, par):
                order.enter(b)
                if present(b, 2):
                    power(0, b + 2, ve1, mv1, rs1)
                if present(b, 1):
                    split_T(b + 1, 1 - par, b if present(b, -1) else 0)
                if present(b, -1):
                    normalize(b - 1)
                if present(b, 1):
                    split_N(b + 1, 1 - par)
                if present(b, 2):
                    power(1, b + 2, ve2, mv2, rs2)
                    residual(b + 2, par)
                if present(b, -1):
                    ffn_input(b - 1)

            batches(pool, body)
            order.enter(B)
            ffn_input(B - 1)

        @block.scalar
        def _(act):
            def self_exp(n, par):
                act.wait_ge(smax_done, n + 1)
                nc.scalar.activation(sc[par][:, :], sc[par][:, :], ACT.Exp, bias=nsmax[par][:, :],
                                     accum_out=ssum[par][:, :]).then_inc(sexp_done, 1)

            def high_N(n, par, part):
                if part == 0:
                    act.wait_ge(ctx_in_s, (n + 1) * 48)
                    at_least(act, pv_done, (n - 1) * STEPS)
                if part < PARTS - 1:
                    chunks = slice(part * FULL // (PARTS - 1), (part + 1) * FULL // (PARTS - 1))
                    nc.scalar.activation(cN_hi[par][:, chunks, 0:DC], cN_raw[:, chunks, :], ACT.Copy)
                else:
                    nc.scalar.activation(last_hi[:, :], cN_raw[0:ROWS, FULL, :], ACT.Copy).then_inc(cNhi_done, 1)

            def high_q(n, par, j, use, bank):
                act.wait_ge(misc_ready, use + 1)
                nc.scalar.activation(q_hi[par][0:DC, j * BLK:(j + 1) * BLK], banks[0:DC, bank, 0:BLK],
                                     ACT.Copy).then_inc(qhi_done, 1)

            def evacuate(n, pair, y_use=None):
                act.wait_ge(pv_done, n * STEPS + (pair + 1) * NCH)
                if y_use is not None:
                    act.wait_ge(misc_ready, y_use + 1)
                nc.scalar.activation(o_sb[:, pair * PAIR:(pair + 1) * PAIR].rearrange("p (a q) -> p a q", a=2),
                                     banks[0:DC + 1, OUT:OUT + 2, 0:BLK], ACT.Copy).then_inc(o_evac, 1)

            def g_bank(j):
                act.wait_ge(mg_ready, 5 + j)
                nc.scalar.activation(G[:, 4 * j:4 * j + 4, :],
                                     banks[0:DC, GBANKS[j], :].rearrange("p (h d) -> p h d", h=4),
                                     ACT.Copy).then_inc(g_done, 1)

            for j in range(4):
                if 1 <= j <= 2:
                    self_exp(j - 1, j - 1)
                act.wait_ge(mg_ready, j + 1)
                nc.scalar.activation(M[:, 4 * j:4 * j + 4, :],
                                     banks[:, j, 0:4 * DC].rearrange("p (h d) -> p h d", h=4),
                                     ACT.Copy).then_inc(m_done, 1)
            act.wait_ge(const_s, NCONST // 2 + 2)
            for j in range(QB):
                k = START.index(("q", j))
                high_q(0, 0, j, k, MISC + k % 2)
                if j < 2:
                    g_bank(j)
            for part in range(PARTS):
                high_N(0, 0, part)
            g_bank(2)
            g_bank(3)
            act.wait_ge(const_s, NCONST)

            def body(b, par):
                at = body_uses(b)
                for s in range(STEPS):
                    n = b * STEPS + s
                    pair = banks[:, ST + 2 * (s % 2):ST + 2 * (s % 2) + 2, 0:BLK]
                    act.wait_ge(st_ready, n + 1)
                    at_least(act, lo_done, n - 1)
                    nc.scalar.activation(pr[:, s % 2, :].rearrange("p (a q) -> p a q", a=2), pair, ACT.Exp,
                                         scale=float(DH) ** -0.5).then_inc(exp_done, 1)
                    at_least(act, pv_done, n - RING + 1)
                    nc.scalar.activation(pr_hi[:, s % RING, :].rearrange("p (a q) -> p a q", a=2), pair, ACT.Exp,
                                         scale=float(DH) ** -0.5).then_inc(hi_done, 1)
                    if s == LAG - 1 and present(b, -1):
                        evacuate(b - 1, NP - 1)
                    if s == NCH + LAG - 1:
                        evacuate(b, 0, use_of(b, "y") if present(b, -1) else None)
                    for what, j, away, use, bank in at[s]:
                        if what == "q":
                            high_q(b + 1, 1 - par, j, use, bank)
                    if present(b, 1) and 3 <= s < 3 + PARTS:
                        high_N(b + 1, 1 - par, s - 3)
                    if s == 6 and present(b, 2):
                        self_exp(b + 2, par)

            batches(act, body)
            evacuate(B - 1, NP - 1)

        @block.vector
        def _(dve):
            order = Order(dve, vchain, 10)
            order.base = 0
            link = order.link

            def stats(st, x):
                order.mark(nc.vector.bn_stats(st[:, :], x))

            def aggregate(i, st, mv):
                nc.vector.bn_aggr(mv[:, :], st[:, :]).then_inc(stats_done[i], 1)

            def normalized(i, n, dst, x, mv, rs, done):
                dve.wait_ge(rstd_done[i], n + 1)
                return nc.vector.tensor_scalar(dst, x, mv[:, 0:1], rs[:, :], ALU.subtract, ALU.mult).then_inc(done, 1)

            def row(n):
                return X[:, bass.ds(n, 1), :].rearrange("p a d -> p (a d)")

            def consume(n, par, what, j, use, bank):
                dve.wait_ge(misc_ready, use + 1)
                here = banks[:, bank, :]
                if what == "q":
                    dve.wait_ge(qhi_done, n * QB + j + 1)
                    nc.vector.tensor_tensor(q_lo[par][:, j * BLK:(j + 1) * BLK], here[0:DC, 0:BLK],
                                            q_hi[par][0:DC, j * BLK:(j + 1) * BLK].bitcast(F32),
                                            ALU.subtract).then_inc(misc_free, 1)
                elif what == "max":
                    t, p = divmod(j, PIECES)
                    nc.vector.tensor_reduce(maxes[:, t, p:p + 1], here[:, 0:PW], AX.X,
                                            ALU.max).then_inc(misc_free, 1)
                    if j == QT * PIECES - 1:
                        dve.wait_ge(misc_free, use + 1)
                        nc.vector.tensor_reduce(negmax[:, :], maxes[:, :, :], AX.X, ALU.max,
                                                negate=True).then_inc(negmax_done, 1)
                elif what == "max_b":
                    t, p = divmod(j, PIECES)
                    nc.vector.tensor_reduce(maxes[:, t, p:p + 1], here[:, 0:PW], AX.X,
                                            ALU.max).then_inc(misc_free, 1)
                    if j == QT * PIECES - 1:
                        dve.wait_ge(misc_free, use + 1)
                        nc.vector.tensor_reduce(negmax[:, FIRST:QT], maxes[:, FIRST:QT, :], AX.X, ALU.max,
                                                negate=True).then_inc(negmax_done, 1)
                elif what == "negmax_a":
                    nc.vector.tensor_copy(negmaxT[0:FIRST, :], here[0:FIRST, 0:P]).then_inc(misc_free, 1)
                elif what == "negmax_b":
                    dve.wait_ge(row_a_in_s, 16)
                    nc.vector.tensor_copy(negmaxT[0:QT - FIRST, :], here[0:QT - FIRST, 0:P]).then_inc(misc_free, 1)
                elif what == "negmax":
                    at_least(dve, row_in_s, n * 32)
                    nc.vector.tensor_copy(negmaxT[:, :], here[0:QT, 0:P]).then_inc(misc_free, 1)
                elif what == "T1":
                    nc.vector.tensor_copy(xnT[par][:, :], here[:, 0:S]).then_inc(misc_free, 1)
                elif what == "QK":
                    v = here[:, 0:4 * S].rearrange("p (a m s) -> p a m s", a=2, m=2)
                    at_least(dve, rope_done, n)
                    order.mark(nc.vector.tensor_tensor(rt[:, :, :], v[:, :, 0, :],
                                                       cosT[:, :].unsqueeze(1).to_broadcast([D, 2, S]), ALU.mult))
                    nc.vector.tensor_tensor(rt2[:, :, :], v[:, :, 1, :],
                                            sinT[:, :].unsqueeze(1).to_broadcast([D, 2, S]),
                                            ALU.mult).then_inc(misc_free, 1)
                    dve.wait_ge(misc_free, use + 1)
                    order.wait()
                    nc.vector.tensor_tensor(qk[par][:, :, :], rt[:, :, :], rt2[:, :, :], ALU.add).then_inc(rope_done, 1)
                elif what == "V":
                    nc.vector.tensor_copy(V[par][:, :], here[0:S, 0:D]).then_inc(misc_free, 1)
                elif what == "S":
                    nc.vector.scalar_tensor_tensor(out=sc[par][:, :], in0=here[0:S, 0:S], scalar=float(D) ** -0.5,
                                                   in1=mask[:, :], op0=ALU.mult, op1=ALU.add).then_inc(misc_free, 1)
                    dve.wait_ge(misc_free, use + 1)
                    nc.vector.tensor_reduce(nsmax[par][:, :], sc[par][:, :], AX.X, ALU.max,
                                            negate=True).then_inc(smax_done, 1)
                elif what == "PT":
                    nc.vector.tensor_copy(prT[par][:, :], here[0:S, 0:S]).then_inc(misc_free, 1)
                    dve.wait_ge(sexp_done, n + 1)
                    order.mark(nc.vector.reciprocal(rsum[par][:, :], ssum[par][:, :]))
                elif what == "AO":
                    order.wait()
                    nc.vector.scalar_tensor_tensor(out=x1[par][:, :], in0=here[0:S, 0:D], scalar=rsum[par][:, :],
                                                   in1=row(n), op0=ALU.mult, op1=ALU.add).then_inc(misc_free, 1)
                    dve.wait_ge(misc_free, use + 1)
                    stats(st2, x1[par][:, :])
                elif what == "T2":
                    nc.vector.tensor_copy(x2T[par][:, :], here[:, 0:S]).then_inc(misc_free, 1)
                elif what == "y":
                    dve.wait_ge(x1b_done, n + 1)
                    nc.vector.tensor_tensor(x2[:, :], here[0:S, 0:D], row(n), ALU.add).then_inc(misc_free, 1)
                    dve.wait_ge(misc_free, use + 1)
                    stats(st3, x2[:, :])
                elif what == "sums":
                    nc.vector.reciprocal(rT[:, j * H // NP:(j + 1) * H // NP], here[0:S, 0:H // NP]).then_inc(misc_free, 1)
                elif what == "yh":
                    dve.wait_ge(misc_free, use)
                    dve.wait_ge(x1b_done, n + 1)
                    for i in range(4):
                        h = 4 * j + i
                        step = nc.vector.scalar_tensor_tensor(
                            out=x2[:, :] if h == H - 1 else acc[:, :], in0=here[0:S, i * D:(i + 1) * D],
                            scalar=rT[:, h:h + 1], in1=row(n) if h == 0 else acc[:, :], op0=ALU.mult, op1=ALU.add)
                        if i < 3:
                            link(step)
                    step.then_inc(misc_free, 1)
                    if h == H - 1:
                        dve.wait_ge(misc_free, use + 1)
                        stats(st3, x2[:, :])
                elif what == "T3":
                    nc.vector.tensor_copy(xdT[:, :], here[:, 0:S]).then_inc(misc_free, 1)
                elif what == "F":
                    dve.wait_ge(x2b_done, n + 1)
                    at_least(dve, out_s, n * 16)
                    nc.vector.tensor_tensor(result[par][:, :], here[0:S, 0:D], x2b[:, :], ALU.add).then_inc(misc_free, 1)

            def quantize(part):
                if part == 0:
                    order.wait()
                    link(nc.vector.tensor_scalar(xneg[:, :], xq[:, :], scl[:, 3:4], 0.0, ALU.mult, ALU.min))
                    link(nc.vector.tensor_scalar(xq[:, :], xq[:, :], scl[:, 3:4], 0.0, ALU.mult, ALU.max))
                elif part == 1:
                    link(nc.vector.scalar_tensor_tensor(out=xq[:, :], in0=xq[:, :], scalar=QMAX, in1=xneg[:, :],
                                                        op0=ALU.min, op1=ALU.add))
                    link(nc.vector.tensor_scalar(xq[:, :], xq[:, :], -QMAX, MAGIC, ALU.max, ALU.add))
                else:
                    nc.vector.tensor_scalar(xq[:, :], xq[:, :], MAGIC, scl[:, 2:3], ALU.subtract,
                                            ALU.mult).then_inc(xd_done, 1)

            def high_T(n, par, half):
                if half == 0:
                    dve.wait_ge(ctx_in_s, (n + 1) * 48)
                    at_least(dve, st_ready, (n - 1) * STEPS)
                keys = slice(half * NT // 2, (half + 1) * NT // 2)
                nc.vector.tensor_copy(cT_hi[par][0:DC, keys], cT_raw[:, keys]).then_inc(cThi_done, 1)

            def last_chunk(n, par):
                dve.wait_ge(cNhi_done, n + 1)
                nc.vector.scalar_tensor_tensor(out=cN_hi[par][0:ROWS, FULL, 0:DC], in0=last_hi[:, :].bitcast(F32),
                                               scalar=last[0:ROWS, 0:1], in1=cN_raw[0:ROWS, FULL, :],
                                               op0=ALU.mult, op1=ALU.add).then_inc(last_done, 1)

            def normalize3(n):
                dve.wait_ge(rstd_done[2], n + 1)
                order.mark(nc.vector.tensor_scalar(xq[:, :], x2[:, :], mv3[:, 0:1], rs3[:, :], ALU.subtract, ALU.mult))

            def start(what, n):
                k = START.index((what, n))
                if what == "q":
                    consume(0, 0, what, n, k, MISC + k % 2)
                else:
                    consume(n, n, what, 0, k, MISC + k % 2)

            dve.wait_ge(x_in_s, 16)
            for n in (0, 1):
                if n:
                    dve.wait_ge(rstd_done[0], 1)
                    dve.wait_ge(xn1_done, 1)
                stats(st1, X[:, n, :])
                order.wait()
                aggregate(0, st1, mv1)
                normalized(0, n, xn1[n][:, :], X[:, n, :], mv1, rs1, xn1_done)
            for what, n in START[:2]:
                start(what, n)
            dve.wait_ge(self_in_s, 16 * 3)
            for what, n in START[2:8]:
                start(what, n)
            dve.wait_ge(const_s, NCONST // 2 + 2)
            high_T(0, 0, 0)
            high_T(0, 0, 1)
            for what, n in START[8:10]:
                start(what, n)
            order.wait()
            start("AO", 0)
            order.wait()
            aggregate(1, st2, mv2)
            normalized(1, 0, xn2[0][:, :], x1[0][:, :], mv2, rs2, xn2_done)
            for use in (("T2", 0), ("q", 0), ("q", 1)):
                start(*use)
            for t in range(FIRST):
                dve.wait_ge(max0_ready, t + 1)
                nc.vector.tensor_reduce(maxes[:, t, 0:1], banks[:, PIECES * (t % 2):PIECES * (t % 2) + PIECES, 0:PW],
                                        AX.XY, ALU.max).then_inc(max0_done, 1)
                if t in BETWEEN:
                    start(*BETWEEN[t])
                    if BETWEEN[t] == ("AO", 1):
                        order.wait()
                        dve.wait_ge(xn2_done, 1)
                        aggregate(1, st2, mv2)
                elif t == 5:
                    last_chunk(0, 0)
                elif t == 3:
                    normalized(1, 1, xn2[1][:, :], x1[1][:, :], mv2, rs2, xn2_done)
            dve.wait_ge(max0_done, FIRST)
            nc.vector.tensor_scalar(negmax[:, 0:FIRST], maxes[:, 0:FIRST, 0], -1.0, None,
                                    ALU.mult).then_inc(negmax_a_done, 1)
            start("negmax_a", 0)
            dve.wait_ge(ffn_in_s, 16 * 4)
            nc.vector.tensor_scalar(wffn[:, :], tern[:, :], 1.0, None, ALU.subtract).then_inc(wffn_done, 1)
            link(nc.vector.tensor_scalar(scl[:, 1:2], scl[:, 0:1], 0.0, None, ALU.mult))
            link(nc.vector.tensor_scalar(scl[:, 3:4], scl[:, 0:1], 1e-5, scl[:, 1:2], ALU.max, ALU.add))
            link(nc.vector.reciprocal(scl[:, 3:4], scl[:, 3:4]))
            link(nc.vector.tensor_scalar(scl[:, 2:3], scl[:, 0:1], 1e-5, FLT_MAX, ALU.max, ALU.min))
            dve.wait_ge(x_rest_s, 16)
            dve.wait_ge(const_s, NCONST)

            def body(b, par):
                at = body_uses(b)
                order.enter(b)
                for s in range(STEPS):
                    n = b * STEPS + s
                    whats = [what for what, *_ in at[s]]
                    if s == 0 and present(b, 1):
                        high_T(b + 1, 1 - par, 0)
                        high_T(b + 1, 1 - par, 1)
                    if present(b, 2):
                        if s == 0:
                            stats(st1, row(b + 2))
                        if s == 2:
                            normalized(0, b + 2, xn1[par][:, :], row(b + 2), mv1, rs1, xn1_done)
                        if s == 13:
                            normalized(1, b + 2, xn2[par][:, :], x1[par][:, :], mv2, rs2, xn2_done)
                    if present(b, -1):
                        if s == 15:
                            normalize3(b - 1)
                        if 16 <= s <= 18:
                            quantize(s - 16)
                    for what, j, away, use, bank in at[s]:
                        if what not in LATE:
                            consume(b + away, par if away % 2 == 0 else 1 - par, what, j, use, bank)
                    y_before = s > 0 and "y" in [what for what, *_ in at[s - 1]]
                    if s == 0 or "AO" in whats or y_before:
                        order.wait()
                    dve.wait_ge(exp_done, n + 1)
                    dve.wait_ge(hi_done, n + 1)
                    at_least(dve, pv_done, n - RING + 1)
                    if chunk(s) < FULL:
                        low, rows = pr_lo, slice(0, P)
                    else:
                        low, rows = pr_hi, slice(LOW_AT, LOW_AT + REST)
                    nc.vector.tensor_tensor(low[rows, s % RING, :], pr[rows, s % 2, :],
                                            pr_hi[rows, s % RING, :].bitcast(F32), ALU.subtract).then_inc(lo_done, 1)
                    if s == 10 and present(b, 1):
                        last_chunk(b + 1, 1 - par)
                    if s == 0 and present(b, 2):
                        aggregate(0, st1, mv1)
                    if "AO" in whats:
                        aggregate(1, st2, mv2)
                    if y_before:
                        aggregate(2, st3, mv3)
                    if s == 3 and present(b, -1):
                        dve.wait_ge(sums_in_s, b * 16)
                        nc.vector.reciprocal(rsums[:, :], sums[:, :]).then_inc(recip_done, 1)
                    for what, j, away, use, bank in at[s]:
                        if what in LATE:
                            consume(b + away, par if away % 2 == 0 else 1 - par, what, j, use, bank)

            batches(dve, body)
            order.enter(B)
            for k, (what, j) in enumerate(TAIL):
                if what == "T3":
                    order.wait()
                    aggregate(2, st3, mv3)
                    normalize3(B - 1)
                    for part in range(3):
                        quantize(part)
                consume(B - 1, 1, what, j, base(B) + k, MISC + (base(B) + k) % 2)

        @block.tensor
        def _(pe):
            def fill(n, par, what, j, use, bank, behind):
                if behind in INPUT.get(what, ()):
                    pe.wait_ge(misc_free, use)
                else:
                    at_least(pe, misc_free, use - 1)
                here = banks[:, bank, :]
                if what == "q":
                    for i in range(4):
                        h = 4 * j + i
                        mm = nc.tensor.matmul(here[0:DC, i * S:(i + 1) * S], M[:, h, :], x2T[par][:, :],
                                              start=True, stop=True)
                elif what == "max":
                    t, p = divmod(j, PIECES)
                    if j == 0:
                        pe.wait_ge(cThi_done, 2 * (n + 1))
                    bank_of = [(qtile(i) + P - 1) // BLK for i in range(QT)]
                    if p == 0 and (t == 0 or bank_of[t] > bank_of[t - 1]):
                        pe.wait_ge(qhi_done, n * QB + bank_of[t] + 1)
                    mm = nc.tensor.matmul(here[:, 0:PW], q_hi[par][0:DC, qtile(t):qtile(t) + P],
                                          cT_hi[par][0:DC, PAT[p]:PAT[p] + PW], start=True, stop=True)
                elif what == "max_b":
                    t, p = divmod(j, PIECES)
                    mm = nc.tensor.matmul(here[:, 0:PW], q_hi[par][0:DC, qtile(t):qtile(t) + P],
                                          cT_hi[par][0:DC, PAT[p]:PAT[p] + PW], start=True, stop=True)
                elif what == "negmax_a":
                    pe.wait_ge(negmax_a_done, 1)
                    mm = nc.tensor.transpose(here[0:FIRST, 0:P], negmax[:, 0:FIRST], ident[:, :])
                elif what == "negmax_b":
                    pe.wait_ge(negmax_done, 1)
                    mm = nc.tensor.transpose(here[0:QT - FIRST, 0:P], negmax[:, FIRST:QT], ident[:, :])
                elif what == "negmax":
                    pe.wait_ge(negmax_done, n + 1)
                    mm = nc.tensor.transpose(here[0:QT, 0:P], negmax[:, :], ident[:, :])
                elif what == "T1":
                    pe.wait_ge(xn1_done, n + 1)
                    mm = nc.tensor.transpose(here[:, 0:S], xn1[par][:, :], ident[0:S, 0:S])
                elif what == "QK":
                    for m in range(4):
                        mm = nc.tensor.matmul(here[:, m * S:(m + 1) * S], wself[:, m, :], xnT[par][:, :],
                                              start=True, stop=True)
                elif what == "V":
                    mm = nc.tensor.matmul(here[0:S, 0:D], xnT[par][:, :], wself[:, 4, :], start=True, stop=True)
                elif what == "S":
                    pe.wait_ge(rope_done, n + 1)
                    mm = nc.tensor.matmul(here[0:S, 0:S], qk[par][:, 0, :], qk[par][:, 1, :], start=True, stop=True)
                elif what == "PT":
                    pe.wait_ge(sexp_done, n + 1)
                    mm = nc.tensor.transpose(here[0:S, 0:S], sc[par][:, :], ident[0:S, 0:S])
                elif what == "AO":
                    mm = nc.tensor.matmul(here[0:S, 0:D], prT[par][:, :], V[par][:, :], start=True, stop=True)
                elif what == "T2":
                    pe.wait_ge(xn2_done, n + 1)
                    mm = nc.tensor.transpose(here[:, 0:S], xn2[par][:, :], ident[0:S, 0:S])
                elif what == "y":
                    pe.wait_ge(on_done, n + 1)
                    for h in range(H):
                        mm = nc.tensor.matmul(here[0:S, 0:D], o_sb[0:DC, h * S:(h + 1) * S], G[:, h, :],
                                              start=(h == 0), stop=(h == H - 1))
                elif what == "sums":
                    pe.wait_ge(o_evac, n * NP + j + 1)
                    for i in range(H // NP):
                        q0 = (j * H // NP + i) * S
                        mm = nc.tensor.matmul(here[0:S, i:i + 1], o_sb[DC:DC + 1, q0:q0 + S],
                                              cT_hi[par][DC:DC + 1, 0:1].bitcast(F32), start=True, stop=True)
                elif what == "yh":
                    for i in range(4):
                        h = 4 * j + i
                        mm = nc.tensor.matmul(here[0:S, i * D:(i + 1) * D], o_sb[0:DC, h * S:(h + 1) * S], G[:, h, :],
                                              start=True, stop=True)
                elif what == "T3":
                    pe.wait_ge(xd_done, n + 1)
                    mm = nc.tensor.transpose(here[:, 0:S], xq[:, :], ident[0:S, 0:S])
                elif what == "F":
                    if isinstance(n, int):
                        pe.wait_ge(wffn_done, 1)
                    mm = nc.tensor.matmul(here[0:S, 0:D], xdT[:, :], wffn[:, :], start=True, stop=True)
                mm.then_inc(misc_ready, 1)

            def start(what, n):
                k = START.index((what, n))
                behind = START[k - 1][0] if k else None
                if what == "q":
                    fill(0, 0, what, n, k, MISC + k % 2, behind)
                else:
                    fill(n, n, what, 0, k, MISC + k % 2, behind)

            def m_bank(j):
                for i in range(4):
                    mm = nc.tensor.matmul(banks[:, j, i * DC:(i + 1) * DC], wqT[:, 4 * j + i, :],
                                          wkT[:, 4 * j + i, :], start=True, stop=True)
                mm.then_inc(mg_ready, 1)

            def g_bank(j):
                if j == 0:
                    pe.wait_ge(wvo_in_s, 32)
                if j == 2:
                    pe.wait_ge(misc_free, NSTART - 1)
                for i in range(4):
                    mm = nc.tensor.matmul(banks[0:DC, GBANKS[j], i * D:(i + 1) * D], wvT[:, 4 * j + i, :],
                                          wo[:, 4 * j + i, :], start=True, stop=True)
                mm.then_inc(mg_ready, 1)

            pe.wait_ge(const_s, 4)
            start("T1", 0)
            start("T1", 1)
            pe.wait_ge(self_in_s, 16 * 3)
            for what, n in START[2:6]:
                start(what, n)
            pe.wait_ge(wqk_in_s, 32)
            m_bank(0)
            for j, what in enumerate(("S", "PT")):
                start(what, 0)
                start(what, 1)
                m_bank(j + 1)
            start("AO", 0)
            m_bank(3)
            start("T2", 0)
            pe.wait_ge(m_done, 4)
            start("q", 0)
            g_bank(0)
            start("q", 1)
            pe.wait_ge(cThi_done, 2)
            for t in range(FIRST):
                pe.wait_ge(qhi_done, (qtile(t) + P - 1) // BLK + 1)
                at_least(pe, max0_done, t - 1)
                for p in range(PIECES):
                    mm = nc.tensor.matmul(banks[:, PIECES * (t % 2) + p, 0:PW], q_hi[0][0:DC, qtile(t):qtile(t) + P],
                                          cT_hi[0][0:DC, PAT[p]:PAT[p] + PW], start=True, stop=True)
                mm.then_inc(max0_ready, 1)
                if t == 0:
                    g_bank(1)
                    pe.wait_ge(g_done, 2)
                if t in BETWEEN:
                    start(*BETWEEN[t])
                elif t >= FIRST - 2:
                    g_bank(t - FIRST + 4)
            pe.wait_ge(g_done, 4)
            start("negmax_a", 0)
            pe.wait_ge(max0_done, FIRST)
            pe.wait_ge(const_s, NCONST)

            def scores(b, par, s, i):
                pair, c = s // NCH, chunk(s)
                if s == 0 and i == 0:
                    if isinstance(b, int) and b == 0:
                        pe.wait_ge(row_a_in_s, 16)
                    else:
                        pe.wait_ge(row_in_s, (b + 1) * 32)
                    pe.wait_ge(cTlo_done, b + 1)
                if s == NCH and i == 0 and isinstance(b, int) and b == 0:
                    pe.wait_ge(row_in_s, 32)
                if i == 0:
                    at_least(pe, hi_done, b * STEPS + s - 1)
                keys = slice(c * P, (c + 1) * P)
                terms = [(cT_hi[par][0:DC + 1, keys], q_hi[par][0:DC + 1, :]),
                         (cT_hi[par][0:DC, keys], q_lo[par][:, :]),
                         (cT_lo[par][:, keys], q_hi[par][0:DC, :])]
                k, q = terms[i]
                for a in range(2):
                    q0 = pair * PAIR + a * BLK
                    mm = nc.tensor.matmul(banks[:, ST + 2 * (s % 2) + a, 0:BLK], k, q[:, q0:q0 + BLK],
                                          start=(i == 0), stop=(i == 2))
                if i == 2:
                    mm.then_inc(st_ready, 1)

            def values(b, par, s, i):
                pair, c = s // NCH, chunk(s)
                if c == FULL:
                    if i == 0:
                        if s == 0:
                            pe.wait_ge(last_done, b + 1)
                        at_least(pe, o_evac, b * NP + pair)
                        pe.wait_ge(lo_done, b * STEPS + s + 1)
                        for a in range(2):
                            mm = nc.tensor.matmul(banks[0:DC + 1, OUT + a, 0:BLK], cN_hi[par][:, c, 0:DC + 1],
                                                  pr_hi[:, s % RING, a * BLK:(a + 1) * BLK], start=True, stop=False)
                        mm.then_inc(pv_done, 1)
                    return
                if s == 1 and i == 0:
                    pe.wait_ge(cNhi_done, b + 1)
                    pe.wait_ge(cNlo_done, b + 1)
                if i == 0:
                    pe.wait_ge(hi_done, b * STEPS + s + 1)
                if i == 2:
                    pe.wait_ge(lo_done, b * STEPS + s + 1)
                r = s % RING
                terms = [(cN_hi[par][:, c, 0:DC + 1], pr_hi, DC + 1), (cN_lo[par][:, c, :], pr_hi, DC),
                         (cN_hi[par][:, c, 0:DC + 1], pr_lo, DC + 1)]
                k, e, m = terms[i]
                for a in range(2):
                    mm = nc.tensor.matmul(banks[0:m, OUT + a, 0:BLK], k, e[:, r, a * BLK:(a + 1) * BLK],
                                          start=False, stop=(s % NCH == NCH - 1 and i == 2))
                if i == 2:
                    mm.then_inc(pv_done, 1)

            def body(b, par):
                at = body_uses(b)
                behind = None
                for s in range(STEPS):
                    slots = 6
                    for i in range(6):
                        if i < 3:
                            scores(b, par, s, i)
                        elif s >= LAG:
                            values(b, par, s - LAG, i - 3)
                        elif present(b, -1):
                            values(b - 1, 1 - par, STEPS + s - LAG, i - 3)
                        for what, j, away, use, bank in at[s][i * len(at[s]) // slots:(i + 1) * len(at[s]) // slots]:
                            fill(b + away, par if away % 2 == 0 else 1 - par, what, j, use, bank, behind)
                            behind = what

            batches(pe, body)
            for s in range(STEPS - LAG, STEPS):
                for i in range(3):
                    values(B - 1, 1, s, i)
            for k, (what, j) in enumerate(TAIL):
                fill(B - 1, 1, what, j, base(B) + k, MISC + (base(B) + k) % 2, TAIL[k - 1][0] if k else None)


def kernel(x, ctx_768, L0_attn_wq, L0_attn_wk, L0_attn_wv, L0_xattn_Wq, L0_xattn_Wk, L0_xattn_Wv,
           L0_xattn_Wo, L0_xattn_bo, L0_ffn_ternary_weight, L0_ffn_bias, L0_ffn_act_scale):
    import numpy as np
    import concourse.bacc as bacc
    from concourse.bass_utils import run_bass_kernel_spmd

    B, S, D = x.shape
    NK, DC = ctx_768.shape[1:]
    DH = 64
    H = L0_xattn_Wq.shape[1] // DH
    P = 128
    full = NK // P
    ctx = np.asarray(ctx_768)
    rows = np.concatenate([full * P + first + np.arange(keys) for first, keys, _ in COPIES])
    ctx_last = ctx[:, rows]
    ctxT = np.concatenate([ctx[:, :full * P].reshape(B, P, full, DC).transpose(0, 3, 2, 1).reshape(B, DC, full * P),
                           ctx_last.transpose(0, 2, 1)], axis=2)
    last = np.zeros((P, 2), dtype=np.float32)
    last[:len(rows), 0] = np.concatenate([np.full(keys, -1.0 if kind == "lo" else 0.0) for _, keys, kind in COPIES])
    last[:len(rows), 1] = 1.0 + last[:len(rows), 0]
    order = np.concatenate([np.arange(0, D, 2), np.arange(1, D, 2)])
    swapped = np.concatenate([order[D // 2:], order[:D // 2]])
    wq, wk, wv = (np.asarray(w) for w in (L0_attn_wq, L0_attn_wk, L0_attn_wv))
    wself = np.stack([wq[order].T, wq[swapped].T, wk[order].T, wk[swapped].T, wv.T], axis=1)
    i = np.arange(D // 2, dtype=np.float32)
    phi = np.power(np.float32(10000.0), np.float32(-2.0) * (i - np.float32(1.0)) / np.float32(D)).astype(np.float32)
    ang = (phi[:, None] * np.arange(S, dtype=np.float32)[None, :]).astype(np.float32)
    cos, sin = np.cos(ang).astype(np.float32), np.sin(ang).astype(np.float32)

    def by_head(w):
        return np.asarray(w).reshape(w.shape[0], H, DH).transpose(2, 1, 0)

    named = {
        "x": np.asarray(x), "ctx": ctx, "ctx_last": ctx_last, "ctxT": ctxT, "wself": wself,
        "wqT": by_head(L0_xattn_Wq), "wkT": by_head(L0_xattn_Wk), "wvT": by_head(L0_xattn_Wv),
        "wo": np.asarray(L0_xattn_Wo).reshape(H, DH, D).transpose(1, 0, 2),
        "bo": np.asarray(L0_xattn_bo), "tern": np.asarray(L0_ffn_ternary_weight).T,
        "fbias": np.asarray(L0_ffn_bias), "ascale": np.asarray(L0_ffn_act_scale).reshape(1, 1),
        "cos": np.concatenate([cos, cos]), "sin": np.concatenate([sin, -sin]), "last": last,
    }
    nc = bacc.Bacc("TRN2", target_bir_lowering=False, num_devices=1)
    arrays, args = {}, []
    for name, a in named.items():
        a = np.ascontiguousarray(a)
        arrays["in_" + name] = a
        args.append(nc.dram_tensor("in_" + name, a.shape, mybir.dt.from_np(a.dtype), kind="ExternalInput").ap())
    args.append(nc.dram_tensor("out", (B, S, D), mybir.dt.float32, kind="ExternalOutput").ap())
    decoder_layer(nc, *args)
    r = run_bass_kernel_spmd(nc, [arrays], core_ids=[0])
    return r.results[0]["out"]
```
